# Optimizing a Trainium2 kernel written in Bass

```python
import numpy as np
import jax
import jax.numpy as jnp

def _softmax(x, axis=-1):
    return jax.nn.softmax(x, axis=axis)

def _gelu(x):
    return jax.nn.gelu(x, approximate=True)

def _silu(x):
    return jax.nn.silu(x)

def _sigmoid(x):
    return jax.nn.sigmoid(x)

def _layernorm(x, axis=-1, eps=1e-05):
    m = jnp.mean(x, axis=axis, keepdims=True)
    v = jnp.var(x, axis=axis, keepdims=True)
    return (x - m) / jnp.sqrt(v + eps)

def _scatter_add(tgt, idx, src, axis=0):
    return tgt.at[idx].add(src)

def _segment_sum(src, seg, n):
    return jax.ops.segment_sum(src, seg, n)
kernel_name = 'mk_adaln_d1_jaxref_r8_c8486a'

def setup_inputs(seed: int=0):
    np.random.seed(seed)
    _w = jnp.asarray

    def _L0_attn_setup():
        import jax, jax.numpy as jnp
        import numpy as np
        from jax import lax
        D_MODEL = 128
        N_HEADS = 16
        FACTOR = 1
        key = jax.random.key(seed)
        ks = jax.random.split(key, 9)
        B, S, D = (8, 256, D_MODEL)
        x = jax.random.normal(ks[0], (B, S, D), dtype=jnp.float32)
        scale = 1.0 / np.sqrt(D)
        Wq = jax.random.normal(ks[1], (D, D), dtype=jnp.float32) * scale
        Wk = jax.random.normal(ks[2], (D, D), dtype=jnp.float32) * scale
        Wv = jax.random.normal(ks[3], (D, D), dtype=jnp.float32) * scale
        Wo = jax.random.normal(ks[4], (D, D), dtype=jnp.float32) * scale
        bq = jax.random.normal(ks[5], (D,), dtype=jnp.float32) * scale
        bk = jax.random.normal(ks[6], (D,), dtype=jnp.float32) * scale
        bv = jax.random.normal(ks[7], (D,), dtype=jnp.float32) * scale
        bo = jax.random.normal(ks[8], (D,), dtype=jnp.float32) * scale
        return {'x': x, 'Wq': Wq, 'bq': bq, 'Wk': Wk, 'bk': bk, 'Wv': Wv, 'bv': bv, 'Wo': Wo, 'bo': bo}
    _L0_attn_in = _L0_attn_setup()

    def _L0_ffn_setup():
        import jax, jax.numpy as jnp
        import numpy as np
        E = 8
        K = 2
        D = 128
        F = 512
        EPS = 1e-05

        def _layernorm(h, g, b):
            mu = h.mean(axis=-1, keepdims=True)
            var = ((h - mu) ** 2).mean(axis=-1, keepdims=True)
            return (h - mu) * jax.lax.rsqrt(var + EPS) * g[:, None, :] + b[:, None, :]
        key = jax.random.key(seed)
        ks = jax.random.split(key, 8)
        B, S = (2, 256)
        x = jax.random.normal(ks[0], (B, S, D), dtype=jnp.float32)
        Wr = jax.random.normal(ks[1], (D, E), dtype=jnp.float32) / np.sqrt(D)
        br = jnp.zeros((E,), dtype=jnp.float32)
        W1 = jax.random.normal(ks[2], (E, D, F), dtype=jnp.float32) / np.sqrt(D)
        b1 = jnp.zeros((E, F), dtype=jnp.float32)
        g1 = jnp.ones((E, F), dtype=jnp.float32)
        be1 = jnp.zeros((E, F), dtype=jnp.float32)
        W2 = jax.random.normal(ks[3], (E, F, D), dtype=jnp.float32) / np.sqrt(F)
        b2 = jnp.zeros((E, D), dtype=jnp.float32)
        g2 = jnp.ones((E, D), dtype=jnp.float32)
        be2 = jnp.zeros((E, D), dtype=jnp.float32)
        return {'x': x, 'Wr': Wr, 'br': br, 'W1': W1, 'b1': b1, 'g1': g1, 'be1': be1, 'W2': W2, 'b2': b2, 'g2': g2, 'be2': be2}
    _L0_ffn_in = _L0_ffn_setup()
    _L0_c = _w((lambda *s: np.random.randn(*s).astype(np.float32) * 0.05)(8, 128))
    _L0_wmod = _w((lambda *s: np.random.randn(*s).astype(np.float32) * 0.05)(128, 6 * 128) * 128 ** (-0.5))
    _d = {'L0_attn_x': _L0_attn_in['x'], 'L0_attn_Wq': _L0_attn_in['Wq'], 'L0_attn_bq': _L0_attn_in['bq'], 'L0_attn_Wk': _L0_attn_in['Wk'], 'L0_attn_bk': _L0_attn_in['bk'], 'L0_attn_Wv': _L0_attn_in['Wv'], 'L0_attn_bv': _L0_attn_in['bv'], 'L0_attn_Wo': _L0_attn_in['Wo'], 'L0_attn_bo': _L0_attn_in['bo'], 'L0_ffn_Wr': _L0_ffn_in['Wr'], 'L0_ffn_br': _L0_ffn_in['br'], 'L0_ffn_W1': _L0_ffn_in['W1'], 'L0_ffn_b1': _L0_ffn_in['b1'], 'L0_ffn_g1': _L0_ffn_in['g1'], 'L0_ffn_be1': _L0_ffn_in['be1'], 'L0_ffn_W2': _L0_ffn_in['W2'], 'L0_ffn_b2': _L0_ffn_in['b2'], 'L0_ffn_g2': _L0_ffn_in['g2'], 'L0_ffn_be2': _L0_ffn_in['be2'], 'L0_c': _L0_c, 'L0_wmod': _L0_wmod}
    _x0 = _d['L0_attn_x']
    _d['L0_attn_x'] = jax.random.normal(jax.random.fold_in(jax.random.key(seed), 1), (8, 256, 128), dtype=_x0.dtype)
    del _x0
    return _d

def reference(L0_attn_x, L0_attn_Wq, L0_attn_bq, L0_attn_Wk, L0_attn_bk, L0_attn_Wv, L0_attn_bv, L0_attn_Wo, L0_attn_bo, L0_ffn_Wr, L0_ffn_br, L0_ffn_W1, L0_ffn_b1, L0_ffn_g1, L0_ffn_be1, L0_ffn_W2, L0_ffn_b2, L0_ffn_g2, L0_ffn_be2, L0_c, L0_wmod):

    def _L0_attn_ref(x, Wq, bq, Wk, bk, Wv, bv, Wo, bo):
        import jax, jax.numpy as jnp
        import numpy as np
        from jax import lax
        D_MODEL = 128
        N_HEADS = 16
        FACTOR = 1
        B, S, D = x.shape
        H = N_HEADS
        dk = D // H
        topk = S * FACTOR

        def proj(W, b):
            y = x @ W + b
            return y.reshape(B, S, H, dk).transpose(0, 2, 1, 3)
        Q = proj(Wq, bq)
        K = proj(Wk, bk)
        V = proj(Wv, bv)
        qf = jnp.fft.rfft(Q, axis=-2)
        kf = jnp.fft.rfft(K, axis=-2)
        corr = jnp.fft.irfft(qf * jnp.conj(kf), n=S, axis=-2)
        w = lax.top_k(corr.transpose(0, 1, 3, 2), topk)[0]
        w = w.transpose(0, 1, 3, 2)
        w = jax.nn.softmax(w, axis=-2)
        out = jnp.einsum('bhti,bhij->bhtj', w, V[:, :, :dk, :])
        ctx = out.transpose(0, 2, 1, 3).reshape(B, topk, D)
        return ctx @ Wo + bo

    def _L0_ffn_ref(x, Wr, br, W1, b1, g1, be1, W2, b2, g2, be2):
        import jax, jax.numpy as jnp
        import numpy as np
        E = 8
        K = 2
        D = 128
        F = 512
        EPS = 1e-05

        def _layernorm(h, g, b):
            mu = h.mean(axis=-1, keepdims=True)
            var = ((h - mu) ** 2).mean(axis=-1, keepdims=True)
            return (h - mu) * jax.lax.rsqrt(var + EPS) * g[:, None, :] + b[:, None, :]
        B, S, _ = x.shape
        xt = x.reshape(-1, D)
        logits = xt @ Wr + br
        p = jax.nn.softmax(logits, axis=-1)
        probs, idx = jax.lax.top_k(p, K)
        probs = probs / probs.sum(axis=-1, keepdims=True)
        h = jnp.einsum('td,edf->etf', xt, W1) + b1[:, None, :]
        h = _layernorm(jax.nn.relu(h), g1, be1)
        y = jnp.einsum('etf,efd->etd', h, W2) + b2[:, None, :]
        y = _layernorm(jax.nn.relu(y), g2, be2)
        gate = (jax.nn.one_hot(idx, E, dtype=x.dtype) * probs[..., None]).sum(axis=1)
        out = jnp.einsum('te,etd->td', gate, y)
        return out.reshape(B, S, D)
    x = L0_attn_x
    mod = (_silu(L0_c) @ L0_wmod).reshape(L0_c.shape[0], 6, 1, -1)
    sa, ca, ga, sb, cb, gb = (mod[:, 0], mod[:, 1], mod[:, 2], mod[:, 3], mod[:, 4], mod[:, 5])
    ga = (2 * (ga >= 0) - 1) * jnp.maximum(jnp.abs(ga), 0.25)
    gb = (2 * (gb >= 0) - 1) * jnp.maximum(jnp.abs(gb), 0.25)
    h = _layernorm(x, axis=-1) * (1 + ca) + sa
    x = x + ga * _L0_attn_ref(h, L0_attn_Wq, L0_attn_bq, L0_attn_Wk, L0_attn_bk, L0_attn_Wv, L0_attn_bv, L0_attn_Wo, L0_attn_bo)
    h = _layernorm(x, axis=-1) * (1 + cb) + sb
    x = x + gb * _L0_ffn_ref(h, L0_ffn_Wr, L0_ffn_br, L0_ffn_W1, L0_ffn_b1, L0_ffn_g1, L0_ffn_be1, L0_ffn_W2, L0_ffn_b2, L0_ffn_g2, L0_ffn_be2)
    return x

_drawn_inputs = setup_inputs


def setup_inputs(seed=0):
    import zlib

    import numpy as np

    out = dict(_drawn_inputs(seed))
    spreads = {'L0_ffn_br': (0.0, 0.1),
     'L0_ffn_b1': (0.0, 0.298),
     'L0_ffn_g1': (1.0, 0.2),
     'L0_ffn_be1': (0.0, 0.36),
     'L0_ffn_b2': (0.0, 0.373),
     'L0_ffn_g2': (1.0, 0.2),
     'L0_ffn_be2': (0.0, 0.447)}
    factors = {'L0_attn_Wq': 200.0,
     'L0_attn_bq': 200.0,
     'L0_attn_Wk': 200.0,
     'L0_attn_bk': 200.0,
     'L0_attn_bv': 4.787}
    for name, (base, spread) in spreads.items():
        noise = np.random.default_rng([zlib.crc32(name.encode()), seed]).standard_normal(out[name].shape)
        drawn = base * np.exp(spread * noise) if base else spread * noise
        out[name] = jnp.asarray(drawn.astype(out[name].dtype))
    for name, factor in factors.items():
        out[name] = (out[name] * factor).astype(out[name].dtype)
    return out
```

```python
import numpy as np
import concourse.bass as bass
from concourse import mybir
from contextlib import ExitStack

F32 = mybir.dt.float32
BF16 = mybir.dt.bfloat16
I32 = mybir.dt.int32
U32 = mybir.dt.uint32
ALU = mybir.AluOpType
ACT = mybir.ActivationFunctionType
AX = mybir.AxisListType.X

P = 128
B, S, D = 8, 256, 128
H, DK = 16, 8
E, F = 8, 512
TOP = 2
C = S // P
NT = B * C
G = 4
BG = B // G
TG = NT // G
T = B * S
FC = F // P
EPS = 1e-5

NS = (TOP * T + E * (P - 1)) // P
W = D + 2
NF = S + DK

K_ID, K_TRI, K_INV, K_FWD = 0, P, 2 * P, 2 * P + C * S
K_HM = K_FWD + C * NF
K_IOTA = K_HM + H
K_LT = K_IOTA + E
K_Q = K_LT + E * E
K_S = K_Q + T // P
K_M0 = K_S + NS
K_N = K_M0 + 1


def constants():
    c = np.zeros((P, K_N), np.float64)
    c[:, K_ID:K_ID + P] = np.eye(P)
    c[:, K_TRI:K_TRI + P] = np.triu(np.ones((P, P)), 1)
    k, n = np.arange(P)[:, None], np.arange(S)[None, :]
    turn = 2 * np.pi * ((k * n) % S) / S
    sign = 1.0 - 2.0 * (np.arange(S) % 2)
    inv = np.stack([2 * np.cos(turn) / S, 2 * np.sin(turn) / S])
    inv[0, 0] = 1.0 / S
    inv[1, 0] = sign / S
    c[:, K_INV:K_INV + 2 * S] = inv.transpose(1, 0, 2).reshape(P, 2 * S)
    fwd = np.zeros((S, NF))
    fwd[:, :P] = np.cos(turn).T
    fwd[:, P:2 * P] = np.sin(turn).T
    fwd[:, P] = sign
    fwd[:DK, S:] = np.eye(DK)
    c[:, K_FWD:K_FWD + C * NF] = fwd.reshape(C, P, NF).transpose(1, 0, 2).reshape(P, C * NF)
    c[:, K_HM:K_HM + H] = np.arange(P)[:, None] // DK == np.arange(H)[None]
    c[:, K_IOTA:K_IOTA + E] = E - np.arange(E)
    c[:, K_LT:K_LT + E * E] = np.tril(np.ones((E, E)), -1).reshape(-1)
    c[:, K_Q:K_Q + T // P] = P * np.arange(T // P)
    c[:, K_S:K_S + NS] = np.arange(NS)
    c[:, K_M0] = np.arange(P) != 0
    i = np.arange(TOP * NT)[None, :]
    dest = i * P + np.arange(P)[:, None]
    unused = np.zeros((NS * P, W), np.float32)
    unused[:, D] = (TOP * T + np.arange(NS * P)).astype(np.int32).view(np.float32)
    return c.astype(np.float32), dest.astype(np.int32), unused


def build(nc, x, Wq, bq, Wk, bk, Wv, bv, Wo, bo, Wr, br, W1, b1, g1, be1, W2, b2, g2, be2, cond, wmod,
          const, dest, unused, out, pairs, results):
    ctx = ExitStack()
    with ctx:
        def sb(name, shape, dt=F32):
            return ctx.enter_context(nc.sbuf_tensor(name, shape, dt))

        def sem(name):
            return ctx.enter_context(nc.semaphore(name))

        cst = sb("cst", [P, K_N])
        ident = cst[:, K_ID:K_ID + P]
        inv = cst[:, K_INV:K_INV + 2 * S].rearrange("p (r n) -> p r n", r=2)
        fwd = cst[:, K_FWD:K_FWD + C * NF].rearrange("p (c n) -> p c n", c=C)
        headmask = cst[:, K_HM:K_HM + H]
        iota = cst[:, K_IOTA:K_IOTA + E]
        below = cst[:, K_LT:K_LT + E * E].rearrange("p (a b) -> p a b", a=E)
        q128 = cst[:, K_Q:K_Q + T // P]
        siota = cst[:, K_S:K_S + NS]
        not0 = cst[:, K_M0:K_M0 + 1]
        dst = sb("dst", [P, TOP * NT], I32)

        X = sb("X", [P, NT, D])
        xn = sb("xn", [P, NT, D])
        xga = sb("xga", [P, NT, D])
        wqk = sb("wqk", [P, 2 * D])
        wv = sb("wv", [P, D])
        wo = sb("wo", [P, D])
        bqk = sb("bqk", [1, 2 * D])
        bvc = sb("bvc", [P, 1])
        bo8 = sb("bo8", [B, D])
        wr = sb("wr", [P, E])
        brr = sb("brr", [1, E])
        c8 = sb("c8", [B, D])
        wm = sb("wm", [P, 6 * D])
        w1 = sb("w1", [P, E, F])
        w2 = sb("w2", [P, E * FC, D])
        g1r = sb("g1r", [E * FC, P])
        be1r = sb("be1r", [E * FC, P])
        g1c = sb("g1c", [P, E * FC])
        be1c = sb("be1c", [P, E * FC])
        b2r = sb("b2r", [1, E * D])
        g2b = sb("g2b", [P, E, D])
        be2b = sb("be2b", [P, E, D])
        b1w = sb("b1w", [P, E * F // P])
        b1s = sb("b1s", [P, 3, E * F // P], BF16)
        b1t = sb("b1t", [P, 2, E * F // P])
        b1r = sb("b1r", [3, E, F], BF16)

        ones = sb("ones", [P, P])
        onesb = sb("onesb", [P, P], BF16)
        trib = sb("trib", [P, P], BF16)
        eps = sb("eps", [P, 1])

        sg = sb("sg", [P, 4, B])
        modT = sb("modT", [P, 2, B])
        rows = sb("rows", [B, 5, D])
        rowt = sb("rowt", [B, 4, D])
        MB = sb("MB", [P, B, 5, D])
        st = sb("st", [P, NT, 6])
        mv = sb("mv", [P, NT, 2])
        sd = sb("sd", [P, NT])
        rs = sb("rs", [P, NT])
        HF = sb("HF", [P, B, NF])
        QK = sb("QK", [P, B, 2, 2 * D])
        TT = sb("TT", [P, 2, BG, 2, D])
        AD = sb("AD", [P, B, 2, D])
        mx8 = sb("mx8", [P, B, 8])
        nmx = sb("nmx", [P, B])
        ex = xn[:, :, :].rearrange("p t d -> p (t d)").rearrange("p (b n) -> p b n", b=B)
        srt = sb("srt", [P, B, S])
        Z = sb("Z", [P, B])
        rZ = sb("rZ", [P, B])
        over = sb("over", [P, B])
        cnt = sb("cnt", [P, B])
        ovf = sb("ovf", [P, 2])
        flag = sb("flag", [1, 1], I32)
        work = sb("work", [P, 2, S])
        top = sb("top", [P, 8])
        VT = sb("VT", [P, B, DK])
        BD = sb("BD", [P, B, H, DK])
        MM = sb("MM", [P, B, D])
        R = sb("R", [P, TOP, NT, W])
        h2T = X[:, :, :]
        r16 = [sb(f"r16_{n}", [P, NT]) for n in range(12)]
        r128 = [sb(f"r128_{n}", [P, NT, E]) for n in range(12)]
        Mb = sb("Mb", [P, NT, E], BF16)
        Ms = sb("Ms", [P, E], BF16)
        nt = sb("nt", [P, 4, E])
        cmpq = sb("cmpq", [P, E, T // P])
        cmpl = sb("cmpl", [P, E, E])
        cmps = sb("cmps", [P, NS, E])
        es = sb("es", [P, 2, NS])
        etab = sb("etab", [P, NS], I32)
        slots = sb("slots", [P, NT, TOP], U32)
        U = 6
        XG = sb("XG", [P, U, W])
        V = 3
        reuse = QK[:, :, :, :].rearrange("p b c n -> p (b c n)")
        r = reuse[:, 0:V * F].rearrange("p (u n) -> p u n", u=V)
        rT = reuse[:, V * F:2 * V * F].rearrange("p (u c n) -> p u c n", u=V, c=FC)
        xT = reuse[:, 2 * V * F:2 * V * F + V * P].rearrange("p (u n) -> p u n", u=V)
        yr = sb("yr", [P, U, D])
        yo = AD[:, :, :, :].rearrange("p b c n -> p (b c n)")[:, 0:U * 2 * D].rearrange("p (u k d) -> p u k d", u=U, k=2)
        hst = sb("hst", [P, U, 6])
        hmv = sb("hmv", [P, U, 4])
        yst = sb("yst", [P, U, 6])
        ymv = sb("ymv", [P, U, 4])
        Y = QK[:, :, :, :].rearrange("p b c n -> p (b c n)").rearrange("p (k t d) -> p k t d", k=TOP, t=NT)
        x1 = xga

        ps = ctx.enter_context(nc.psum_tensor("ps", [P, 8, 512], F32))

        s_cst, s_c, s_wm, s_attn, s_r = sem("s_cst"), sem("s_c"), sem("s_wm"), sem("s_attn"), sem("s_r")
        s_x = [sem(f"s_x{g}") for g in range(G)]
        s_b2 = sem("s_b2")
        s_w1, s_w2, s_g1, s_g2, s_b1, s_b1r = sem("s_w1"), sem("s_w2"), sem("s_g1"), sem("s_g2"), sem("s_b1"), sem("s_b1r")
        s_padded = sem("s_padded")
        dve, act, pool = sem("dve"), sem("act"), sem("pool")
        ready = sem("ready")
        transposed = sem("transposed")
        silu_in, silu_ex, silu = sem("silu_in"), sem("silu_ex"), sem("silu")
        mod_mm, mod_rows, mod_T = sem("mod_mm"), sem("mod_rows"), sem("mod_T")
        bc_mm, bc_cp = sem("bc_mm"), sem("bc_cp")
        var1, std1, norm1 = sem("var1"), sem("std1"), sem("norm1")
        hf_mm, hf_cp, hf_ok = sem("hf_mm"), sem("hf_cp"), sem("hf_ok")
        qk_mm, qk_cp, qk_dc = sem("qk_mm"), sem("qk_cp"), sem("qk_dc")
        prod, dcfix = sem("prod"), sem("dcfix")
        corr, maxed, exped, topped = sem("corr"), sem("maxed"), sem("exped"), sem("topped")
        ovf_in, ovf_mm, sorted_ = sem("ovf_in"), sem("ovf_mm"), sem("sorted_")
        v_mm, v_cp, bd_ok, m_mm, m_ok = sem("v_mm"), sem("v_cp"), sem("bd_ok"), sem("m_mm"), sem("m_ok")
        o_mm, xga_ok, x1_ok = sem("o_mm"), sem("xga_ok"), sem("x1_ok")
        var2, std2, h2_ok, h2_copied, h2t_mm, h2t_cp = sem("var2"), sem("std2"), sem("h2_ok"), sem("h2_copied"), sem("h2t_mm"), sem("h2t_cp")
        lg_mm, lg_in, lg_ex, mask_ok, pos_mm = sem("lg_mm"), sem("lg_in"), sem("lg_ex"), sem("mask_ok"), sem("pos_mm")
        gates_ok, slots_ok, etab_ok, sent = sem("gates_ok"), sem("slots_ok"), sem("etab_ok"), sem("sent")
        be_mm, b2_ok, w2_ok, b1_split = sem("be_mm"), sem("b2_ok"), sem("w2_ok"), sem("b1_split")
        s_slow = sem("s_slow")
        s_xg = [sem(f"s_xg{u}") for u in range(U)]
        l_xT, l_xTc, l_h, l_relu = sem("l_xT"), sem("l_xTc"), sem("l_h"), sem("l_relu")
        l_hst, l_hvar, l_hstd, l_hrs, l_rn = sem("l_hst"), sem("l_hvar"), sem("l_hstd"), sem("l_hrs"), sem("l_rn")
        l_rT, l_rTc, l_y, l_yrelu = sem("l_rT"), sem("l_rTc"), sem("l_y"), sem("l_yrelu")
        l_yst, l_yvar, l_ystd, l_yrs, l_yn = sem("l_yst"), sem("l_yvar"), sem("l_ystd"), sem("l_yrs"), sem("l_yn")
        l_yg, l_yb, l_yo = sem("l_yg"), sem("l_yb"), sem("l_yo")
        s_res = [sem(f"s_res{u}") for u in range(U)]
        s_y = [sem(f"s_y{g}") for g in range(G)]
        f_sum, f_gb, f_out, s_out = sem("f_sum"), sem("f_gb"), sem("f_out"), sem("s_out")

        class Steps:
            def __init__(self, eng, s):
                self.eng, self.sem, self.n = eng, s, 0

            def mark(self, ins):
                self.n += 1
                ins.then_inc(self.sem, 1)

            def then(self, ins):
                self.mark(ins)
                self.eng.wait_ge(self.sem, self.n)

        x_v = x.rearrange("b (c p) d -> p (b c) d", p=P)
        out_v = out.rearrange("b (c p) d -> p (b c) d", p=P)
        FIRST = U + NS % U
        ROUNDS = (NS - FIRST) // U
        assert FIRST + ROUNDS * U == NS

        def tiles(eng, step, lag):
            for n in range(FIRST):
                if n >= lag:
                    step(n - lag, (n - lag) % U)
            with eng.Fori(0, ROUNDS) as j:
                for u in range(U):
                    k = FIRST + u - lag
                    step(j * U + k, k % U)
            for n in range(NS, NS + lag):
                step(n - lag, (n - lag) % U)

        block = ctx.enter_context(nc.Block())

        @block.sync
        def _(sp):
            sp.dma_start(c8[:, :], cond).then_inc(s_c, 16)
            sp.dma_start(cst[:, :], const).then_inc(s_cst, 16)
            for g in range(G):
                sp.dma_start(X[:, g * TG:(g + 1) * TG, :], x_v[:, g * TG:(g + 1) * TG, :]).then_inc(s_x[g], 16)
            sp.dma_start(wm[:, :], wmod).then_inc(s_wm, 16)
            attn = [(wqk[:, 0:D], Wq), (wqk[:, D:2 * D], Wk), (wv[:, :], Wv), (wo[:, :], Wo),
                    (bqk[:, 0:D], bq.rearrange("(a n) -> a n", a=1)), (bqk[:, D:2 * D], bk.rearrange("(a n) -> a n", a=1)),
                    (bvc[:, :], bv.rearrange("(n a) -> n a", a=1)),
                    (bo8[:, :], bo.rearrange("(a n) -> a n", a=1).broadcast_to([B, D]))]
            for a, b in attn:
                sp.dma_start(a, b).then_inc(s_attn, 16)
            sp.dma_start(wr[:, :], Wr).then_inc(s_r, 16)
            sp.dma_start(brr[:, :], br.rearrange("(a n) -> a n", a=1)).then_inc(s_r, 16)
            sp.dma_start(dst[:, :], dest).then_inc(s_r, 16)
            sp.dma_start(g1r[:, :], g1.rearrange("e (c p) -> (e c) p", p=P)).then_inc(s_g1, 16)
            sp.dma_start(be1r[:, :], be1.rearrange("e (c p) -> (e c) p", p=P)).then_inc(s_g1, 16)
            sp.dma_start(b2r[:, :], b2.rearrange("(a e) d -> a (e d)", a=1)).then_inc(s_b2, 16)
            sp.dma_start(b1w[:, :], b1.rearrange("e (a n) -> (e a) n", n=E * F // P)).then_inc(s_b1, 16)
            sp.dma_start(w2[:, :, :], W2.rearrange("e (c p) d -> p (e c) d", p=P)).then_inc(s_w2, 16)
            sp.dma_start(w1[:, :, :], W1.rearrange("e d f -> d e f")).then_inc(s_w1, 16)
            for a, b in ((g2b, g2), (be2b, be2)):
                row = b.rearrange("(a e) d -> a (e d)", a=1).broadcast_to([P, E * D])
                sp.dma_start(a[:, :, :].rearrange("p e d -> p (e d)"), row).then_inc(s_g2, 16)
            sp.dma_start(pairs, unused).then_inc(s_padded, 16)
            sp.wait_ge(b1_split, 3)
            for k in range(3):
                sp.dma_start(b1r[k:k + 1, :, :].rearrange("a e (q n) -> a (e q) n", n=E * F // P),
                             b1s[:, k, :]).then_inc(s_b1r, 16)
            sp.wait_ge(sent, 16 * TOP * NT)

            for n in range(U):
                sp.dma_start(XG[:, n, :], pairs[n * P:(n + 1) * P, :]).then_inc(s_xg[n], 16)
            with sp.Fori(0, (NS - U) // U) as j:
                for u in range(U):
                    sp.wait_ge(s_res[u], (j + 1) * 16)
                    sp.dma_start(XG[:, u, :], pairs[bass.ds((j * U + (U + u)) * P, P), :]).then_inc(s_xg[u], 16)
            for n in range((NS // U) * U, NS):
                sp.wait_ge(s_res[n % U], (n // U) * 16)
                sp.dma_start(XG[:, n % U, :], pairs[n * P:(n + 1) * P, :]).then_inc(s_xg[n % U], 16)
            for u in range(U):
                sp.wait_ge(s_res[u], 16 * len(range(u, NS, U)))
            for g in range(G):
                for k in range(TOP):
                    sp.dma_start(Y[:, k, g * TG:(g + 1) * TG, :],
                                 results[k * T + g * TG * P:k * T + (g + 1) * TG * P, :]
                                 .rearrange("(t p) d -> p t d", p=P)).then_inc(s_y[g], 16)
            for g in range(G):
                sp.wait_ge(f_out, g + 1)
                sp.dma_start(out_v[:, g * TG:(g + 1) * TG, :], xn[:, g * TG:(g + 1) * TG, :]).then_inc(s_out, 16)
            sp.wait_ge(s_out, 16 * G)

        @block.gpsimd
        def _(gp):
            me = Steps(gp, pool)
            gp.memset(ones[:, :], 1.0).then_inc(ready, 1)
            gp.memset(onesb[:, :], 1.0).then_inc(ready, 1)
            gp.memset(eps[:, :], EPS).then_inc(ready, 1)
            gp.memset(srt[:, :, :], 0.0).then_inc(ready, 1)
            gp.wait_ge(s_r, 48)
            for k in range(TOP):
                me.mark(gp.tensor_copy(R[:, k, :, D].bitcast(I32), dst[:, k * NT:(k + 1) * NT]))
            gp.wait_ge(s_cst, 16)
            me.mark(gp.tensor_copy(trib[:, :], cst[:, K_TRI:K_TRI + P]))
            gp.wait_ge(s_b1, 16)
            me.mark(gp.tensor_copy(b1s[:, 0, :], b1w[:, :]))
            gp.wait_ge(pool, me.n)
            me.then(gp.tensor_tensor(b1t[:, 0, :], b1w[:, :], b1s[:, 0, :], ALU.subtract))
            me.then(gp.tensor_copy(b1s[:, 1, :], b1t[:, 0, :]))
            me.then(gp.tensor_tensor(b1t[:, 1, :], b1t[:, 0, :], b1s[:, 1, :], ALU.subtract))
            gp.tensor_copy(b1s[:, 2, :], b1t[:, 1, :]).then_inc(b1_split, 3)
            gp.wait_ge(s_attn, 16 * 8)
            me.then(gp.tensor_scalar(bqk[:, :], bqk[:, :], float(S), None, ALU.mult))
            for g in range(G):
                gp.wait_ge(qk_cp, (g + 1) * BG)
                v = QK[0:1, g * BG:(g + 1) * BG, 0, :]
                gp.tensor_tensor(v, v, bqk[:, :].rearrange("p (a n) -> p a n", a=1).broadcast_to([1, BG, 2 * D]),
                                 ALU.add).then_inc(qk_dc, 1)
                gp.wait_ge(bc_cp, 2 * (g + 1) * BG)
                gp.wait_ge(s_x[g], 16)
                for b in range(g * BG, (g + 1) * BG):
                    gp.tensor_tensor(xga[:, b * C:(b + 1) * C, :], X[:, b * C:(b + 1) * C, :],
                                     MB[:, b, 1:2, :].broadcast_to([P, C, D]), ALU.add).then_inc(xga_ok, 1)
            gp.wait_ge(v_cp, 1)
            gp.tensor_tensor(BD[:, :, :, :], VT[:, :, :].rearrange("p b (a i) -> p b a i", a=1).broadcast_to([P, B, H, DK]),
                             headmask.rearrange("p (a h b) -> p a h b", a=1, b=1).broadcast_to([P, B, H, DK]),
                             ALU.mult).then_inc(bd_ok, 1)
            gp.wait_ge(be_mm, 2)
            gp.wait_ge(transposed, 1)
            gp.tensor_tensor(w2[:, :, :], w2[:, :, :],
                             g1c[:, :].rearrange("p (n a) -> p n a", a=1).broadcast_to([P, E * FC, D]),
                             ALU.mult).then_inc(w2_ok, 1)
            gp.wait_ge(slots_ok, 1)
            gp.wait_ge(gates_ok, 2)
            gp.wait_ge(h2_copied, 1)
            gp.wait_ge(s_padded, 16)
            gp.wait_ge(pool, me.n)
            for i in range(NT):
                for k in range(TOP):
                    gp.indirect_dma_start(pairs, bass.IndirectOffsetOnAxis(slots[:, i, k:k + 1], 0),
                                          R[:, k, i, :], None).then_inc(sent, 16)

            gp.wait_ge(etab_ok, 1)
            gp.wait_ge(s_g2, 32)

            def send(t, u):
                gp.indirect_dma_start(results, bass.IndirectOffsetOnAxis(XG[:, u, D:D + 1].bitcast(U32), 0),
                                      yo[:, u, 1, :], None).then_inc(s_res[u], 16)

            def scale(t, u):
                e = gp.value_load(etab[0:1, bass.ds(t, 1)], min_val=0, max_val=E - 1)
                gp.wait_ge(l_yn, t + 1)
                gp.tensor_tensor(yo[:, u, 0, :], yr[:, u, :], g2b[:, bass.ds(e, 1), :].rearrange("p a d -> p (a d)"),
                                 ALU.mult).then_inc(l_yg, 1)
                before = not isinstance(t, int) or t >= 1
                if before:
                    gp.wait_ge(l_yo, t)
                gp.wait_ge(l_yg, t + 1)
                gp.tensor_tensor(yo[:, u, 0, :], yo[:, u, 0, :], be2b[:, bass.ds(e, 1), :].rearrange("p a d -> p (a d)"),
                                 ALU.add).then_inc(l_yb, 1)
                if before:
                    send(t - 1, (u - 1) % U)
                gp.wait_ge(l_yb, t + 1)
                gp.tensor_tensor(yo[:, u, 1, :], yo[:, u, 0, :], XG[:, u, D + 1:D + 2].broadcast_to([P, D]),
                                 ALU.mult).then_inc(l_yo, 1)

            tiles(gp, scale, 3)
            gp.wait_ge(l_yo, NS)
            send(NS - 1, (NS - 1) % U)
            for g in range(G):
                for b in range(g * BG, (g + 1) * BG):
                    gp.wait_ge(f_sum, b + 1)
                    gp.tensor_tensor(Y[:, 0, b * C:(b + 1) * C, :], Y[:, 0, b * C:(b + 1) * C, :],
                                     MB[:, b, 4:5, :].broadcast_to([P, C, D]), ALU.mult).then_inc(f_gb, 1)

        @block.scalar
        def _(ac):
            a = nc.scalar.activation
            ac.wait_ge(ready, 4)
            ac.wait_ge(transposed, 1)
            a(sg[:, 1, :], ps[:, 7, 0:B], ACT.Exp, scale=-1.0).then_inc(silu_ex, 1)
            nc.scalar.copy(sg[:, 0, :], ps[:, 7, 0:B]).then_inc(silu_in, 1)
            nc.scalar.copy(g1c[:, :], ps[:, 7, 32:64]).then_inc(silu_in, 1)
            nc.scalar.copy(be1c[:, :], ps[:, 7, 64:96]).then_inc(silu_in, 1)

            def std_first(g):
                ac.wait_ge(var1, g + 1)
                a(sd[:, g * TG:(g + 1) * TG], mv[:, g * TG:(g + 1) * TG, 1], ACT.Sqrt, bias=eps[:, :]).then_inc(std1, 1)

            std_first(0)
            for g in range(G):
                if g + 1 < G:
                    std_first(g + 1)
                if g == 0:
                    ac.wait_ge(mod_T, 1)
                for b in range(g * BG, (g + 1) * BG):
                    ac.wait_ge(hf_mm, b + 1)
                    a(HF[:, b, :], ps[:, b % 2, 0:NF], ACT.Identity, scale=modT[:, 1, b:b + 1]).then_inc(hf_cp, 1)
                for b in range((g - 1) * BG, g * BG) if g else ():
                    ac.wait_ge(qk_mm, b + 1)
                    nc.scalar.copy(QK[:, b, :, :].rearrange("p c n -> p (c n)"), ps[:, 2 + b % 2, :]).then_inc(qk_cp, 1)
            for b in range((G - 1) * BG, B):
                ac.wait_ge(qk_mm, b + 1)
                nc.scalar.copy(QK[:, b, :, :].rearrange("p c n -> p (c n)"), ps[:, 2 + b % 2, :]).then_inc(qk_cp, 1)
            for b in range(B):
                ac.wait_ge(bc_mm, b + 1)
                nc.scalar.copy(MB[:, b, 0:4, :].rearrange("p k d -> p (k d)"), ps[:, 6, :]).then_inc(bc_cp, 1)
                nc.scalar.copy(MB[:, b, 4, :], ps[:, 7, 384:512]).then_inc(bc_cp, 1)
            ac.wait_ge(v_mm, 1)
            a(VT[:, :, :].rearrange("p b i -> p (b i)"), ps[:, 7, 0:B * DK], ACT.Identity, bias=bvc[:, :]).then_inc(v_cp, 1)
            for b in range(B):
                ac.wait_ge(maxed, b // 2 * 2 + 2)
                a(ex[:, b, :], ps[:, 4 + (b // 2) % 2, (b % 2) * S:(b % 2 + 1) * S], ACT.Exp, bias=nmx[:, b:b + 1],
                  accum_out=Z[:, b:b + 1]).then_inc(exped, 1)
                a(srt[:, b, 0:8], mx8[:, b, :], ACT.Exp, bias=nmx[:, b:b + 1]).then_inc(topped, 1)
            for g in range(G):
                t0, t1 = g * TG, (g + 1) * TG
                ac.wait_ge(var2, g + 1)
                a(sd[:, t0:t1], mv[:, t0:t1, 1], ACT.Sqrt, bias=eps[:, :]).then_inc(std2, 1)
            for g in range(G):
                ac.wait_ge(h2t_mm, g + 1)
                nc.scalar.copy(h2T[:, g * TG:(g + 1) * TG, :].rearrange("p t d -> p (t d)"), ps[:, 4 + g, :]).then_inc(h2t_cp, 1)
            nc.scalar.copy(R[:, 1, :, 0:D], R[:, 0, :, 0:D]).then_inc(h2_copied, 1)
            ac.wait_ge(lg_in, 1)
            a(r128[1][:, :, :], r128[0][:, :, :], ACT.Exp).then_inc(lg_ex, 1)
            def front(t, u):
                ac.wait_ge(l_xT, t + 1)
                nc.scalar.copy(xT[:, u % V, :], ps[:, 6 + u % 2, 0:P]).then_inc(l_xTc, 1)
                ac.wait_ge(l_h, t + 1)
                a(r[:, u % V, :], ps[:, u % 2, :], ACT.Relu).then_inc(l_relu, 1)

            def hstd(t, u):
                ac.wait_ge(l_hvar, t + 1)
                a(hmv[:, u, 2:3], hmv[:, u, 1:2], ACT.Sqrt, bias=eps[:, :]).then_inc(l_hstd, 1)

            def back(t, u):
                ac.wait_ge(l_rT, t + 1)
                nc.scalar.copy(rT[:, u % V, :, :].rearrange("p c t -> p (c t)"), ps[:, 2 + u % 2, :]).then_inc(l_rTc, 1)
                ac.wait_ge(l_y, t + 1)
                a(yr[:, u, :], ps[:, 4 + u % 2, 0:D], ACT.Relu).then_inc(l_yrelu, 1)

            def ystd(t, u):
                ac.wait_ge(l_yvar, t + 1)
                a(ymv[:, u, 2:3], ymv[:, u, 1:2], ACT.Sqrt, bias=eps[:, :]).then_inc(l_ystd, 1)

            def step(t, u):
                late = not isinstance(t, int)
                if late or t < NS:
                    front(t, u)
                if late or t >= 3:
                    ystd(t - 3, (u - 3) % U)
                if late or 2 <= t < NS + 2:
                    back(t - 2, (u - 2) % U)
                if late or t < NS:
                    hstd(t, u)

            tiles(ac, step, 0)
            for n in range(NS, NS + 3):
                step(n, n % U)

        @block.vector
        def _(ve):
            me = Steps(ve, dve)
            v = nc.vector

            def layernorm_stats(src, g, var, std):
                t0, t1 = g * TG, (g + 1) * TG
                for t in range(t0, t1):
                    me.mark(v.bn_stats(st[:, t, :], src[:, t, :]))
                ve.wait_ge(dve, me.n)
                for t in range(t0, t1):
                    last = v.bn_aggr(mv[:, t, :], st[:, t, :])
                last.then_inc(var, 1)
                ve.wait_ge(std, g + 1)
                me.then(v.reciprocal(rs[:, t0:t1], sd[:, t0:t1]))

            ve.wait_ge(silu_ex, 1)
            me.then(v.tensor_scalar(sg[:, 2, :], sg[:, 1, :], 1.0, None, ALU.add))
            me.then(v.reciprocal(sg[:, 3, :], sg[:, 2, :]))
            ve.wait_ge(silu_in, 1)
            v.tensor_tensor(sg[:, 1, :], sg[:, 0, :], sg[:, 3, :], ALU.mult).then_inc(silu, 1)

            def add_sa(g):
                b0, b1_ = g * BG, (g + 1) * BG
                ve.wait_ge(hf_cp, b1_)
                me.then(v.scalar_tensor_tensor(HF[:, b0:b1_, 0], modT[:, 0, b0:b1_], float(S), HF[:, b0:b1_, 0], ALU.mult, ALU.add))
                v.tensor_tensor(HF[:, b0:b1_, S:NF], HF[:, b0:b1_, S:NF],
                                modT[:, 0, b0:b1_].rearrange("p (b a) -> p b a", a=1).broadcast_to([P, BG, DK]),
                                ALU.add).then_inc(hf_ok, 1)

            for g in range(G):
                ve.wait_ge(s_x[g], 16)
                layernorm_stats(X, g, var1, std1)
                for t in range(g * TG, (g + 1) * TG):
                    last = v.tensor_scalar(xn[:, t, :], X[:, t, :], mv[:, t, 0:1], rs[:, t:t + 1], ALU.subtract, ALU.mult)
                last.then_inc(norm1, 1)
                if g == 0:
                    ve.wait_ge(mod_mm, 1)
                    me.mark(v.tensor_copy(modT[:, 0, :], ps[:, 7, 128:128 + B]))
                    v.tensor_scalar(modT[:, 1, :], ps[:, 7, 128 + B:128 + 2 * B], 1.0, None, ALU.add).then_inc(mod_T, 1)
                    ve.wait_ge(s_attn, 16 * 8)
                    for k, src in ((0, ps[0:B, 6, 0:D]), (4, ps[0:B, 6, 3 * D:4 * D])):
                        me.mark(v.tensor_scalar(rowt[:, 0, :], src, 0.0, 2.0, ALU.is_ge, ALU.mult))
                        me.then(v.tensor_scalar(rowt[:, 2, :], src, -1.0, 0.25, ALU.mult, ALU.max))
                        me.then(v.tensor_tensor(rowt[:, 1, :], rowt[:, 2, :], src, ALU.max))
                        me.then(v.scalar_tensor_tensor(rows[:, k, :], rowt[:, 0, :], -1.0, rowt[:, 1, :], ALU.add, ALU.mult))
                    me.mark(v.tensor_tensor(rows[:, 1, :], rows[:, 0, :], bo8[:, :], ALU.mult))
                    me.mark(v.tensor_scalar(rows[:, 2, :], ps[0:B, 6, 2 * D:3 * D], 1.0, None, ALU.add))
                    me.then(v.tensor_copy(rows[:, 3, :], ps[0:B, 6, D:2 * D]))
                    v.tensor_copy(rowt[:, 3, 0:1], rows[:, 3, 0:1]).then_inc(mod_rows, 1)
                else:
                    add_sa(g - 1)
            add_sa(G - 1)

            def corr_max(b):
                ve.wait_ge(corr, b // 2 * 2 + 2)
                bank = 4 + (b // 2) % 2
                me.then(v.max(mx8[:, b, :], ps[:, bank, (b % 2) * S:(b % 2 + 1) * S]))
                v.tensor_scalar(nmx[:, b:b + 1], mx8[:, b, 0:1], -1.0, None, ALU.mult).then_inc(maxed, 1)

            for g in range(G):
                b0, b1_ = g * BG, (g + 1) * BG
                ve.wait_ge(qk_dc, g + 1)
                if g:
                    ve.wait_ge(dcfix, g)
                for r_ in range(2):
                    me.mark(v.tensor_tensor(TT[:, r_, :, :, :], QK[:, b0:b1_, :, 0:D],
                                            QK[:, b0:b1_, r_:r_ + 1, D:2 * D].broadcast_to([P, BG, 2, D]), ALU.mult))
                ve.wait_ge(dve, me.n)
                me.mark(v.scalar_tensor_tensor(AD[:, b0:b1_, 0, :], TT[:, 1, :, 1, :], not0, TT[:, 0, :, 0, :], ALU.mult, ALU.add))
                me.then(v.tensor_tensor(AD[:, b0:b1_, 1, :], TT[:, 0, :, 1, :], TT[:, 1, :, 0, :], ALU.subtract))
                v.tensor_copy(AD[0:1, b0:b1_, 1, :], TT[0:1, 1, :, 1, :]).then_inc(dcfix, 1)
                if g:
                    for b in range((g - 1) * BG, b0):
                        corr_max(b)
            for b in range((G - 1) * BG, B):
                corr_max(b)
            for b in range(B):
                ve.wait_ge(exped, b + 1)
                me.mark(v.tensor_scalar(work[:, b % 2, :], ex[:, b, :], 0.0, 0.0, ALU.is_gt, ALU.add, accum_out=cnt[:, b:b + 1]))
                if b:
                    ve.wait_ge(dve, me.n - 1)
            ve.wait_ge(dve, me.n)
            me.mark(v.reciprocal(rZ[:, :], Z[:, :]))
            me.then(v.tensor_reduce(ovf[:, 0:1], cnt[:, :], AX, ALU.max))
            v.tensor_scalar(ovf[:, 1:2], ovf[:, 0:1], 8.0, None, ALU.is_gt).then_inc(ovf_in, 1)
            for b in range(B):
                ve.wait_ge(m_mm, b // 4 + 1)
                v.scalar_tensor_tensor(MM[:, b, :], ps[:, 6 + b // 4, (b % 4) * D:(b % 4 + 1) * D], rZ[:, b:b + 1],
                                       MB[:, b, 0, :], ALU.mult, ALU.mult).then_inc(m_ok, 1)
            ve.wait_ge(be_mm, 2)
            ve.wait_ge(s_b2, 16)
            v.tensor_tensor(b2r[:, :].rearrange("p (a n) -> p a n", a=2), b2r[:, :].rearrange("p (a n) -> p a n", a=2), ps[0:1, 2:4, :], ALU.add).then_inc(b2_ok, 1)
            ve.wait_ge(ovf_mm, 1)
            me.then(v.tensor_copy(flag[:, :], ps[0:1, 0, 0:1]))
            ve.wait_ge(topped, B)
            some = ve.value_load(flag[0:1, 0:1], min_val=0, max_val=P)
            with ve.If(some > 0):
                with ve.Fori(0, B) as b:
                    v.tensor_copy(work[:, 0, :], ex[:, bass.ds(b, 1), :].rearrange("p a n -> p (a n)"))
                    v.tensor_copy(top[:, :], srt[:, bass.ds(b, 1), 0:8].rearrange("p a n -> p (a n)"))
                    ve.drain()
                    with ve.Fori(0, S // 8 - 1) as k:
                        v.match_replace(work[:, 0, :], in_to_replace=top[:, :], in_values=work[:, 0, :], imm_value=-1.0)
                        ve.drain()
                        v.max(top[:, :], work[:, 0, :])
                        ve.drain()
                        v.tensor_copy(srt[:, bass.ds(b, 1), bass.ds(k * 8 + 8, 8)].rearrange("p a n -> p (a n)"), top[:, :])
                        ve.drain()
            v.memset(flag[:, :], 0).then_inc(sorted_, 1)
            for g in range(G):
                t0, t1 = g * TG, (g + 1) * TG
                ve.wait_ge(o_mm, g + 1)
                ve.wait_ge(xga_ok, (g + 1) * BG)
                me.then(v.tensor_tensor(x1[:, t0:t1, :].rearrange("p t d -> p (t d)"),
                                        xga[:, t0:t1, :].rearrange("p t d -> p (t d)"), ps[:, g, :], ALU.add))
                layernorm_stats(x1, g, var2, std2)
                for t in range(t0, t1):
                    me.mark(v.tensor_scalar(R[:, 0, t, 0:D], x1[:, t, :], mv[:, t, 0:1], rs[:, t:t + 1], ALU.subtract, ALU.mult))
                ve.wait_ge(dve, me.n)
                for b in range(g * BG, (g + 1) * BG):
                    z = R[:, 0, b * C:(b + 1) * C, 0:D]
                    me.then(v.tensor_tensor(z, z, MB[:, b, 2:3, :].broadcast_to([P, C, D]), ALU.mult))
                    last = v.tensor_tensor(z, z, MB[:, b, 3:4, :].broadcast_to([P, C, D]), ALU.add)
                last.then_inc(h2_ok, 1)

            def over_e(a):
                return a[:, :].rearrange("p (t a) -> p t a", a=1).broadcast_to([P, NT, E])

            iotb = iota.rearrange("p (a e) -> p a e", a=1).broadcast_to([P, NT, E])
            lg = ps[:, 0, 0:NT * E].rearrange("p (t e) -> p t e", t=NT)
            ve.wait_ge(lg_mm, 1)
            me.then(v.tensor_reduce(r16[0][:, :], lg, AX, ALU.max))
            v.tensor_tensor(r128[0][:, :, :], lg, over_e(r16[0]), ALU.subtract).then_inc(lg_in, 1)
            ve.wait_ge(lg_ex, 1)
            me.then(v.tensor_reduce(r16[1][:, :], r128[1][:, :, :], AX, ALU.add))
            me.then(v.reciprocal(r16[2][:, :], r16[1][:, :]))
            me.then(v.tensor_tensor(r128[2][:, :, :], r128[1][:, :, :], over_e(r16[2]), ALU.mult))

            def largest(p, m, eq, score, k, hot):
                me.then(v.tensor_reduce(m[:, :], p[:, :, :], AX, ALU.max))
                me.then(v.tensor_tensor(eq[:, :, :], p[:, :, :], over_e(m), ALU.is_equal))
                me.then(v.tensor_tensor(score[:, :, :], eq[:, :, :], iotb, ALU.mult))
                me.then(v.tensor_reduce(k[:, :], score[:, :, :], AX, ALU.max))
                me.then(v.tensor_tensor(hot[:, :, :], iotb, over_e(k), ALU.is_equal))

            m1, m2, hot1, hot2 = r16[3], r16[4], r128[3], r128[4]
            largest(r128[2], m1, r128[5], r128[6], r16[5], hot1)
            me.then(v.scalar_tensor_tensor(r128[7][:, :, :], hot1[:, :, :], -2.0, r128[2][:, :, :], ALU.mult, ALU.add))
            largest(r128[7], m2, r128[8], r128[9], r16[6], hot2)
            me.then(v.tensor_tensor(Mb[:, :, :], hot1[:, :, :], hot2[:, :, :], ALU.add))
            with nc.allow_low_precision("counts up to 16 are exact in bf16"):
                v.tensor_reduce(Ms[:, :], Mb[:, :, :].rearrange("p t e -> p e t"), AX, ALU.add).then_inc(mask_ok, 1)
            me.then(v.tensor_tensor(r16[7][:, :], m1[:, :], m2[:, :], ALU.add))
            me.then(v.reciprocal(r16[8][:, :], r16[7][:, :]))
            v.tensor_tensor(R[:, 0, :, D + 1], m1[:, :], r16[8][:, :], ALU.mult).then_inc(gates_ok, 1)
            v.tensor_tensor(R[:, 1, :, D + 1], m2[:, :], r16[8][:, :], ALU.mult).then_inc(gates_ok, 1)
            ve.wait_ge(pos_mm, 1)
            cntp = ps[:, 1, 256:256 + E]
            me.then(v.tensor_tensor(cmpq[:, :, :], cntp.rearrange("p (e a) -> p e a", a=1).broadcast_to([P, E, T // P]),
                                    q128.rearrange("p (a q) -> p a q", a=1).broadcast_to([P, E, T // P]), ALU.is_gt))
            me.then(v.tensor_reduce(nt[:, 0, :], cmpq[:, :, :], AX, ALU.add))
            me.then(v.tensor_tensor(cmpl[:, :, :], below, nt[:, 0:1, :].broadcast_to([P, E, E]), ALU.mult))
            me.then(v.tensor_reduce(nt[:, 1, :], cmpl[:, :, :], AX, ALU.add))
            me.mark(v.tensor_tensor(nt[:, 2, :], nt[:, 1, :], nt[:, 0, :], ALU.add))
            me.then(v.scalar_tensor_tensor(r128[10][:, :, :], nt[:, 1:2, :].broadcast_to([P, NT, E]), float(P),
                                           ps[:, 1, 0:NT * E].rearrange("p (t e) -> p t e", t=NT), ALU.mult, ALU.add))
            for k, hot in enumerate((hot1, hot2)):
                me.then(v.tensor_tensor(r128[11][:, :, :], hot[:, :, :], r128[10][:, :, :], ALU.mult))
                me.then(v.tensor_reduce(r16[9][:, :], r128[11][:, :, :], AX, ALU.add))
                me.then(v.tensor_copy(slots[:, :, k], r16[9][:, :]))
            me.mark(v.memset(flag[:, :], 0))
            v.memset(ovf[:, :], 0.0).then_inc(slots_ok, 1)
            me.then(v.tensor_tensor(cmps[:, :, :], siota.rearrange("p (s a) -> p s a", a=1).broadcast_to([P, NS, E]),
                                    nt[:, 2:3, :].broadcast_to([P, NS, E]), ALU.is_ge))
            me.then(v.tensor_reduce(es[:, 0, :], cmps[:, :, :], AX, ALU.add))
            me.then(v.tensor_scalar(es[:, 1, :], es[:, 0, :], float(E - 1), None, ALU.min))
            v.tensor_copy(etab[:, :], es[:, 1, :]).then_inc(etab_ok, 1)
            def step(t, u, hid=True):
                late = not isinstance(t, int)
                if hid:
                    ve.wait_ge(l_relu, t + 1)
                    v.bn_stats(hst[:, u, :], r[:, u % V, :]).then_inc(l_hst, 1)
                h, y, z = (u - 1) % U, (u - 2) % U, (u - 3) % U
                has_h, has_y, has_z = late or 1 <= t <= NS, late or 2 <= t <= NS + 1, late or 3 <= t
                if has_h:
                    ve.wait_ge(l_hstd, t)
                    v.reciprocal(hmv[:, h, 3:4], hmv[:, h, 2:3]).then_inc(l_hrs, 1)
                if has_y:
                    ve.wait_ge(l_yrelu, t - 1)
                    v.bn_stats(yst[:, y, :], yr[:, y, :]).then_inc(l_yst, 1)
                if has_z:
                    ve.wait_ge(l_ystd, t - 2)
                    v.reciprocal(ymv[:, z, 3:4], ymv[:, z, 2:3]).then_inc(l_yrs, 1)
                if hid:
                    ve.wait_ge(l_hst, t + 1)
                if has_h:
                    ve.wait_ge(l_hrs, t)
                    v.tensor_scalar(r[:, h % V, :], r[:, h % V, :], hmv[:, h, 0:1], hmv[:, h, 3:4],
                                    ALU.subtract, ALU.mult).then_inc(l_rn, 1)
                if hid:
                    v.bn_aggr(hmv[:, u, 0:2], hst[:, u, :]).then_inc(l_hvar, 1)
                if has_y:
                    ve.wait_ge(l_yst, t - 1)
                if has_z:
                    ve.wait_ge(l_yrs, t - 2)
                    v.tensor_scalar(yr[:, z, :], yr[:, z, :], ymv[:, z, 0:1], ymv[:, z, 3:4],
                                    ALU.subtract, ALU.mult).then_inc(l_yn, 1)
                if has_y:
                    v.bn_aggr(ymv[:, y, 0:2], yst[:, y, :]).then_inc(l_yvar, 1)

            tiles(ve, step, 0)
            for n in range(NS, NS + 3):
                step(n, n % U, False)
            def final(b):
                ve.wait_ge(f_gb, b + 1)
                ins = v.tensor_tensor(xn[:, b * C:(b + 1) * C, :], Y[:, 0, b * C:(b + 1) * C, :], x1[:, b * C:(b + 1) * C, :], ALU.add)
                if b % BG == BG - 1:
                    ins.then_inc(f_out, 1)

            for b in range(B):
                ve.wait_ge(s_y[b // BG], 32)
                v.tensor_tensor(Y[:, 0, b * C:(b + 1) * C, :], Y[:, 0, b * C:(b + 1) * C, :], Y[:, 1, b * C:(b + 1) * C, :],
                                ALU.add).then_inc(f_sum, 1)
                if b:
                    final(b - 1)
            final(B - 1)

        @block.tensor
        def _(pe):
            mm = nc.tensor.matmul
            tr = nc.tensor.transpose
            pe.wait_ge(s_cst, 16)
            pe.wait_ge(s_c, 16)
            pe.wait_ge(s_g1, 32)
            tr(ps[:, 7, 0:B], c8[:, :], cst[0:B, K_ID:K_ID + B])
            tr(ps[:, 7, 32:64], g1r[:, :], cst[0:E * FC, K_ID:K_ID + E * FC])
            tr(ps[:, 7, 64:96], be1r[:, :], cst[0:E * FC, K_ID:K_ID + E * FC]).then_inc(transposed, 1)
            pe.wait_ge(silu, 1)
            pe.wait_ge(silu_in, 3)
            pe.wait_ge(s_wm, 16)
            mm(ps[:, 7, 128:128 + B], wm[:, 0:D], sg[:, 1, :], start=True, stop=True)
            mm(ps[:, 7, 128 + B:128 + 2 * B], wm[:, D:2 * D], sg[:, 1, :], start=True, stop=True)
            mm(ps[0:B, 6, :], sg[:, 1, :], wm[:, 2 * D:6 * D], start=True, stop=True).then_inc(mod_mm, 1)

            def transform(b):
                pe.wait_ge(norm1, b // BG + 1)
                if b >= 2:
                    pe.wait_ge(hf_cp, b - 1)
                for c in range(C):
                    n = NF if c == 0 else S
                    ins = mm(ps[:, b % 2, 0:n], xn[:, b * C + c, :], fwd[:, c, 0:n], start=c == 0, stop=c == C - 1,
                             skip_group_check=True)
                ins.then_inc(hf_mm, 1)

            def project(b):
                if b == 0:
                    pe.wait_ge(s_attn, 16 * 8)
                pe.wait_ge(hf_ok, b // BG + 1)
                if b >= 2:
                    pe.wait_ge(qk_cp, b - 1)
                for c in range(2):
                    ins = mm(ps[:, 2 + b % 2, c * 2 * D:(c + 1) * 2 * D], HF[:, b, c * P:(c + 1) * P], wqk[:, :],
                             start=True, stop=True)
                ins.then_inc(qk_mm, 1)

            for g in range(G):
                for b in range(g * BG, (g + 1) * BG):
                    transform(b)
                for b in range((g - 1) * BG, g * BG) if g else ():
                    project(b)
            for b in range((G - 1) * BG, B):
                project(b)
            pe.wait_ge(mod_rows, 1)
            for b in range(B):
                one = cst[0:B, K_ID + b:K_ID + b + 1].broadcast_to([B, P])
                if b:
                    pe.wait_ge(bc_cp, 2 * b)
                mm(ps[:, 6, :], one, rows[:, 0:4, :].rearrange("p k d -> p (k d)"), start=True, stop=True)
                mm(ps[:, 7, 384:512], one, rows[:, 4, :], start=True, stop=True).then_inc(bc_mm, 1)

            pe.wait_ge(bc_cp, 2 * B)
            mm(ps[:, 7, 0:B * DK], wv[:, :], HF[:, :, S:NF], start=True, stop=True).then_inc(v_mm, 1)
            for b in range(B):
                pe.wait_ge(dcfix, b // BG + 1)
                if b >= 4 and b % 2 == 0:
                    pe.wait_ge(exped, b - 2)
                for k in range(2):
                    ins = mm(ps[:, 4 + (b // 2) % 2, (b % 2) * S:(b % 2 + 1) * S], AD[:, b, k, :], inv[:, k, :],
                             start=k == 0, stop=k == 1)
                ins.then_inc(corr, 1)
            pe.wait_ge(bd_ok, 1)
            pe.wait_ge(bc_cp, 2 * B)
            for b in range(B):
                ins = mm(ps[:, 6 + b // 4, (b % 4) * D:(b % 4 + 1) * D], BD[:, b, :, :].rearrange("p h i -> p (h i)"), wo[:, :],
                         start=True, stop=True)
                if b % 4 == 3:
                    ins.then_inc(m_mm, 1)
            pe.wait_ge(silu_in, 3)
            pe.wait_ge(s_w2, 16)
            pe.wait_ge(qk_cp, B)
            for e in range(E):
                for c in range(FC):
                    ins = mm(ps[0:1, 2 + e // 4, (e % 4) * D:(e % 4 + 1) * D], be1c[:, e * FC + c:e * FC + c + 1],
                             w2[:, e * FC + c, :], start=c == 0, stop=c == FC - 1)
                if e % 4 == 3:
                    ins.then_inc(be_mm, 1)
            pe.wait_ge(ovf_in, 1)
            mm(ps[0:1, 0, 0:1], ovf[:, 1:2], ones[:, 0:1], start=True, stop=True).then_inc(ovf_mm, 1)
            pe.wait_ge(sorted_, 1)
            pe.wait_ge(m_ok, B)
            pe.wait_ge(b2_ok, 1)
            for i in range(NT):
                b, c = i // C, i % C
                bank = i // 4
                ins = mm(ps[:, (0, 1, 2, 3)[bank], (i % 4) * D:(i % 4 + 1) * D], srt[:, b, c * P:(c + 1) * P], MM[:, b, :],
                         start=True, stop=True)
                if i % 4 == 3:
                    ins.then_inc(o_mm, 1)
            for g in range(G):
                pe.wait_ge(h2_ok, g + 1)
                for i in range(g * TG, (g + 1) * TG):
                    ins = tr(ps[:, 4 + g, (i % TG) * D:(i % TG + 1) * D], R[:, 0, i, 0:D], ident)
                ins.then_inc(h2t_mm, 1)
            pe.wait_ge(s_r, 48)
            for i in range(NT):
                pe.wait_ge(h2t_cp, i // TG + 1)
                o = ps[:, 0, i * E:(i + 1) * E]
                mm(o, h2T[:, i, :], wr[:, :], start=True, stop=False)
                ins = mm(o, ones[0:1, :], brr[:, :], start=False, stop=True)
            ins.then_inc(lg_mm, 1)
            pe.wait_ge(mask_ok, 1)
            mm(ps[:, 1, 256:256 + E], onesb[:, :], Ms[:, :], start=True, stop=True)
            mm(ps[:, 1, 0:NT * E], trib[:, :], Mb[:, :, :].rearrange("p t e -> p (t e)"), start=True, stop=False, skip_group_check=True)
            for j in range(NT - 1):
                ins = mm(ps[:, 1, (j + 1) * E:NT * E], onesb[:, :],
                         Mb[:, j:j + 1, :].broadcast_to([P, NT - 1 - j, E]), start=False, stop=j == NT - 2,
                         skip_group_check=True)
            ins.then_inc(pos_mm, 1)

            pe.wait_ge(etab_ok, 1)
            pe.wait_ge(s_w1, 16)
            pe.wait_ge(w2_ok, 1)
            pe.wait_ge(b2_ok, 1)
            pe.wait_ge(s_b1r, 48)

            def front(t, u, filled):
                e = pe.value_load(etab[0:1, bass.ds(t, 1)], min_val=0, max_val=E - 1)
                pe.wait_ge(s_xg[u], filled * 16)
                tr(ps[:, 6 + u % 2, 0:P], XG[:, u, 0:D], ident).then_inc(l_xT, 1)
                if not isinstance(t, int) or t >= 2:
                    pe.wait_ge(l_relu, t - 1)
                mm(ps[:, u % 2, :], onesb[0:3, :], b1r[:, bass.ds(e, 1), :].rearrange("p a n -> p (a n)"), start=True, stop=False)
                pe.wait_ge(l_xTc, t + 1)
                mm(ps[:, u % 2, :], xT[:, u % V, :], w1[:, bass.ds(e, 1), :].rearrange("p a n -> p (a n)"),
                   start=False, stop=True).then_inc(l_h, 1)

            def back(t, u):
                e = pe.value_load(etab[0:1, bass.ds(t, 1)], min_val=0, max_val=E - 1)
                pe.wait_ge(l_rn, t + 1)
                for c in range(FC):
                    ins = tr(ps[:, 2 + u % 2, c * P:(c + 1) * P], r[:, u % V, c * P:(c + 1) * P], ident)
                ins.then_inc(l_rT, 1)
                if not isinstance(t, int) or t >= 2:
                    pe.wait_ge(l_yrelu, t - 1)
                o = ps[:, 4 + u % 2, 0:D]
                mm(o, ones[0:1, :], b2r[:, bass.ds(e * D, D)], start=True, stop=False)
                pe.wait_ge(l_rTc, t + 1)
                for c in range(FC):
                    ins = mm(o, rT[:, u % V, c, :], w2[:, bass.ds(e * FC + c, 1), :].rearrange("p a d -> p (a d)"),
                             start=False, stop=c == FC - 1)
                ins.then_inc(l_y, 1)

            for n in range(FIRST):
                front(n, n % U, n // U + 1)
                if n >= 2:
                    back(n - 2, (n - 2) % U)
            with pe.Fori(0, ROUNDS) as j:
                for k in range(U):
                    u = (FIRST + k) % U
                    t = j * U + (FIRST + k)
                    front(t, u, j + ((FIRST + k) // U + 1))
                    back(t - 2, (u - 2) % U)
            for n in (NS - 2, NS - 1):
                back(n, n % U)


_INS = ['L0_attn_x', 'L0_attn_Wq', 'L0_attn_bq', 'L0_attn_Wk', 'L0_attn_bk', 'L0_attn_Wv', 'L0_attn_bv', 'L0_attn_Wo',
        'L0_attn_bo', 'L0_ffn_Wr', 'L0_ffn_br', 'L0_ffn_W1', 'L0_ffn_b1', 'L0_ffn_g1', 'L0_ffn_be1', 'L0_ffn_W2',
        'L0_ffn_b2', 'L0_ffn_g2', 'L0_ffn_be2', 'L0_c', 'L0_wmod']


def kernel(**inputs):
    from concourse import bacc
    from concourse.bass_utils import run_bass_kernel_spmd

    nc = bacc.Bacc("TRN2", target_bir_lowering=False, num_devices=1)
    table, dest, unused = constants()
    arrays = {f"in_{n}": np.ascontiguousarray(inputs[n]) for n in _INS}
    arrays["const"], arrays["dest"], arrays["unused"] = table, dest, unused
    args = [nc.dram_tensor(n, a.shape, mybir.dt.from_np(a.dtype), kind="ExternalInput").ap() for n, a in arrays.items()]
    out = nc.dram_tensor("out", [B, S, D], F32, kind="ExternalOutput").ap()
    pairs = nc.dram_tensor("pairs", [NS * P, W], F32).ap()
    results = nc.dram_tensor("results", [TOP * T + NS * P, D], F32).ap()
    build(nc, *args, out, pairs, results)
    r = run_bass_kernel_spmd(nc, [arrays], core_ids=[0])
    return r.results[0]["out"]
```

```python
import numpy as np
import concourse.bass as bass
from concourse import mybir
from contextlib import ExitStack

F32 = mybir.dt.float32
BF16 = mybir.dt.bfloat16
I32 = mybir.dt.int32
U32 = mybir.dt.uint32
ALU = mybir.AluOpType
ACT = mybir.ActivationFunctionType
AX = mybir.AxisListType.X
TENSOR, POOL = mybir.EngineType.PE, mybir.EngineType.Pool

P = 128
B, S, D = 8, 256, 128
H, DK = 16, 8
E, F = 8, 512
TOP = 2
C = S // P
NT = B * C
G = 4
BG = B // G
TG = NT // G
T = B * S
FC = F // P
EPS = 1e-5

NS_MIN = TOP * T // P
NS = (TOP * T + E * (P - 1)) // P
ND = NS - NS_MIN
RS = T + P
W = D + 2
NF = S + DK

HALF = 2
BH, TH, GH = B // HALF, NT // HALF, G // HALF

U = 6
FIRST = U + (NS - 1) % U
ROUNDS = (NS - FIRST) // U
LOOPED = FIRST + ROUNDS * U
NR = NS // U + 1
RW = U + 2
NE = NR * U + U

K_ID, K_TRI, K_INV, K_FWD = 0, P, 2 * P, 2 * P + C * S
K_HM = K_FWD + C * NF
K_IOTA = K_HM + H
K_LT = K_IOTA + E
K_Q = K_LT + E * E
K_S = K_Q + T // P
K_M0 = K_S + NE
K_RS = K_M0 + 1
K_N = K_RS + E

A_C, A_MOD, A_N = 0, B, B + 6 * D
B_QK, B_V, B_O, B_R = 0, 2 * D, 3 * D, 4 * D
B_BV = B_R + E
B_G1 = B_BV + 1
B_BE1 = B_G1 + E * FC
B_B1 = B_BE1 + E * FC
B_N = B_B1 + E * F // P


def constants():
    c = np.zeros((P, K_N), np.float64)
    c[:, K_ID:K_ID + P] = np.eye(P)
    c[:, K_TRI:K_TRI + P] = np.triu(np.ones((P, P)), 1)
    k, n = np.arange(P)[:, None], np.arange(S)[None, :]
    turn = 2 * np.pi * ((k * n) % S) / S
    sign = 1.0 - 2.0 * (np.arange(S) % 2)
    inv = np.stack([2 * np.cos(turn) / S, 2 * np.sin(turn) / S])
    inv[0, 0] = 1.0 / S
    inv[1, 0] = sign / S
    c[:, K_INV:K_INV + 2 * S] = inv.transpose(1, 0, 2).reshape(P, 2 * S)
    fwd = np.zeros((S, NF))
    fwd[:, :P] = np.cos(turn).T
    fwd[:, P:2 * P] = np.sin(turn).T
    fwd[:, P] = sign
    fwd[:DK, S:] = np.eye(DK)
    c[:, K_FWD:K_FWD + C * NF] = fwd.reshape(C, P, NF).transpose(1, 0, 2).reshape(P, C * NF)
    c[:, K_HM:K_HM + H] = np.arange(P)[:, None] // DK == np.arange(H)[None]
    c[:, K_IOTA:K_IOTA + E] = E - np.arange(E)
    c[:, K_LT:K_LT + E * E] = np.tril(np.ones((E, E)), -1).reshape(-1)
    c[:, K_Q:K_Q + T // P] = P * np.arange(T // P)
    c[:, K_S:K_S + NE] = np.arange(NE)
    c[:, K_M0] = np.arange(P) != 0
    c[:, K_RS:K_RS + E] = RS * np.arange(E)
    i = np.arange(TOP * NT)[None, :]
    dest = i * P + np.arange(P)[:, None]
    unused = np.zeros(((E + ND) * P, W), np.float32)
    unused[:, D] = (TOP * T + np.arange((E + ND) * P)).astype(np.int32).view(np.float32)
    return c.astype(np.float32), dest.astype(np.int32), unused


def build(nc, x, packa, packb, rowpack, bo, br, W1, W2, g2, be2, const, dest, unused, out, modrows, pairs, results):
    ctx = ExitStack()
    with ctx:
        def sb(name, shape, dt=F32):
            return ctx.enter_context(nc.sbuf_tensor(name, shape, dt))

        def sem(name):
            return ctx.enter_context(nc.semaphore(name))

        cst = sb("cst", [P, K_N])
        ident = cst[:, K_ID:K_ID + P]
        inv = cst[:, K_INV:K_INV + 2 * S].rearrange("p (r n) -> p r n", r=2)
        fwd = cst[:, K_FWD:K_FWD + C * NF].rearrange("p (c n) -> p c n", c=C)
        headmask = cst[:, K_HM:K_HM + H]
        iota = cst[:, K_IOTA:K_IOTA + E]
        below = cst[:, K_LT:K_LT + E * E].rearrange("p (a b) -> p a b", a=E)
        q128 = cst[:, K_Q:K_Q + T // P]
        siota = cst[:, K_S:K_S + NE]
        not0 = cst[:, K_M0:K_M0 + 1]
        dst = sb("dst", [P, TOP * NT], I32)

        X = sb("X", [P, NT, D])
        xn = sb("xn", [P, NT, D])
        xga = sb("xga", [P, NT, D])
        pa = sb("pa", [P, A_N])
        cT, wm = pa[:, A_C:A_C + B], pa[:, A_MOD:A_MOD + 6 * D]
        pb = sb("pb", [P, B_N])
        wqk, wv, wo, wr = (pb[:, o:o + n] for o, n in ((B_QK, 2 * D), (B_V, D), (B_O, D), (B_R, E)))
        bvc = pb[:, B_BV:B_BV + 1]
        g1c, be1c = pb[:, B_G1:B_G1 + E * FC], pb[:, B_BE1:B_BE1 + E * FC]
        b1w = pb[:, B_B1:B_B1 + E * F // P]
        rp = sb("rp", [1, E * D + 2 * D])
        b2r, bqk = rp[:, 0:E * D], rp[:, E * D:E * D + 2 * D]
        bo8 = sb("bo8", [B, D])
        brb = sb("brb", [P, E])
        w1 = sb("w1", [P, E, F])
        w2 = sb("w2", [P, E * FC, D])
        g2b = sb("g2b", [P, E, D])
        be2b = sb("be2b", [P, E, D])
        b1s = sb("b1s", [P, 3, E * F // P], BF16)
        b1t = sb("b1t", [P, 2, E * F // P])
        b1r = sb("b1r", [3, E, F], BF16)
        b2w = sb("b2w", [P, E * D // P])
        b2s = sb("b2s", [P, 3, E * D // P], BF16)
        b2t = sb("b2t", [P, 2, E * D // P])
        b2p = sb("b2p", [3, E * D], BF16)

        ones = sb("ones", [P, P])
        onesb = sb("onesb", [P, P], BF16)
        trib = sb("trib", [P, P], BF16)
        eps = sb("eps", [P, 1])

        sg = sb("sg", [P, 4, B])
        modT = sb("modT", [P, 2, B])
        rows = sb("rows", [B, 5, D])
        rowt = sb("rowt", [B, 4, D])
        MB = sb("MB", [P, B, 5, D])
        st = sb("st", [P, NT, 6])
        mv = sb("mv", [P, NT, 2])
        sd = sb("sd", [P, NT])
        rs = sb("rs", [P, NT])
        nmr = sb("nmr", [P, NT])
        HF = sb("HF", [P, B, NF])
        QK = sb("QK", [P, B, 2, 2 * D])
        TT = sb("TT", [P, 2, BG, 2, D])
        AD = sb("AD", [P, B, 2, D])
        mx8 = sb("mx8", [P, B, 8])
        nmx = sb("nmx", [P, B])
        ex = xn[:, :, :].rearrange("p t d -> p (t d)").rearrange("p (b n) -> p b n", b=B)
        srt = sb("srt", [P, B, S])
        Z = sb("Z", [P, B])
        rZ = sb("rZ", [P, B])
        ovf = sb("ovf", [P, HALF, 2])
        flag = sb("flag", [1, HALF], I32)
        work = sb("work", [P, 2, S])
        top = sb("top", [P, 8])
        VT = sb("VT", [P, B, DK])
        BD = sb("BD", [P, B, H, DK])
        MM = sb("MM", [P, B, D])
        R = sb("R", [P, TOP, NT, W])
        h2T = X[:, :, :]
        lgb = sb("lgb", [P, NT, E])
        m1, m2, k1, k2, dm, ed, e1, g1_ = (sb(f"r16_{n}", [P, NT]) for n in range(8))
        eq1, sc1, hot1, rest, eq2, sc2, hot2, posb = (sb(f"r128_{n}", [P, NT, E]) for n in range(8))
        at = [sb(f"at{k}", [P, NT, E]) for k in range(TOP)]
        atf = [sb(f"atf{k}", [P, NT]) for k in range(TOP)]
        Mb = sb("Mb", [P, NT, E], BF16)
        Ms = sb("Ms", [P, HALF, E], BF16)
        nt = sb("nt", [P, 4, E])
        cmpq = sb("cmpq", [P, E, T // P])
        cmpl = sb("cmpl", [P, E, E])
        cmps = sb("cmps", [1, 2, NE, E])
        es = sb("es", [1, 5, NE])
        etab = sb("etab", [1, NR, RW], I32)
        rowtab = sb("rowtab", [1, NE], I32)
        padf = sb("padf", [1, E])
        padtab = sb("padtab", [1, E], I32)
        slots = sb("slots", [P, NT, TOP], U32)
        XG = sb("XG", [P, U, W])
        V = 3
        reuse = QK[:, :, :, :].rearrange("p b c n -> p (b c n)")
        r = reuse[:, 0:V * F].rearrange("p (u n) -> p u n", u=V)
        rT = reuse[:, V * F:2 * V * F].rearrange("p (u c n) -> p u c n", u=V, c=FC)
        xT = reuse[:, 2 * V * F:2 * V * F + V * P].rearrange("p (u n) -> p u n", u=V)
        meta = sb("meta", [P, U, 2])
        yr = sb("yr", [P, U, D])
        yo = AD[:, :, :, :].rearrange("p b c n -> p (b c n)")[:, 0:U * 2 * D].rearrange("p (u k d) -> p u k d", u=U, k=2)
        hst = sb("hst", [P, U, 6])
        hmv = sb("hmv", [P, U, 4])
        yst = sb("yst", [P, U, 6])
        ymv = sb("ymv", [P, U, 4])
        Y = QK[:, :, :, :].rearrange("p b c n -> p (b c n)").rearrange("p (k t d) -> p k t d", k=TOP, t=NT)
        x1 = xga

        ps = ctx.enter_context(nc.psum_tensor("ps", [P, 8, 512], F32))

        s_cst, s_pa, s_pb, s_rp, s_bo, s_br, s_dst = (sem(n) for n in ("s_cst", "s_pa", "s_pb", "s_rp", "s_bo", "s_br", "s_dst"))
        s_x = [sem(f"s_x{g}") for g in range(G)]
        s_w1, s_w2, s_g2, s_b1r = sem("s_w1"), sem("s_w2"), sem("s_g2"), sem("s_b1r")
        s_modw, s_modr = sem("s_modw"), [sem(f"s_modr{n}") for n in range(2)]
        s_dummy, s_padded = sem("s_dummy"), sem("s_padded")
        dve, act, pool = sem("dve"), sem("act"), sem("pool")
        ready = sem("ready")
        silu_ex, silu = sem("silu_ex"), sem("silu")
        mod_mm, mod_rows, mod_T = sem("mod_mm"), sem("mod_rows"), sem("mod_T")
        var1, std1, norm1 = sem("var1"), sem("std1"), sem("norm1")
        hf_mm, hf_cp, hf_ok = sem("hf_mm"), sem("hf_cp"), sem("hf_ok")
        qk_mm, qk_cp, qk_dc = sem("qk_mm"), sem("qk_cp"), sem("qk_dc")
        prod, dcfix = sem("prod"), sem("dcfix")
        corr, maxed, exped, topped = sem("corr"), sem("maxed"), sem("exped"), sem("topped")
        ovf_in, ovf_mm, sorted_ = sem("ovf_in"), sem("ovf_mm"), sem("sorted_")
        v_mm, v_cp, bd_ok, m_mm, m_ok = sem("v_mm"), sem("v_cp"), sem("bd_ok"), sem("m_mm"), sem("m_ok")
        o_mm, xga_ok, x1_ok = sem("o_mm"), sem("xga_ok"), sem("x1_ok")
        var2, std2, rs2_ok, z_ok, h2_ok, h2_copied, h2t_mm, h2t_cp = sem("var2"), sem("std2"), sem("rs2_ok"), sem("z_ok"), sem("h2_ok"), sem("h2_copied"), sem("h2t_mm"), sem("h2t_cp")
        lg_mm, lg_in, lg_ex, mask_ok, pos_mm = sem("lg_mm"), sem("lg_in"), sem("lg_ex"), sem("mask_ok"), sem("pos_mm")
        gates_ok, slots_ok, cnt_mm, pads_ok, etab_ok, sent = sem("gates_ok"), sem("slots_ok"), sem("cnt_mm"), sem("pads_ok"), sem("etab_ok"), sem("sent")
        be_mm, b2_ok, w2_ok, b1_split, b2_split = sem("be_mm"), sem("b2_ok"), sem("w2_ok"), sem("b1_split"), sem("b2_split")
        s_b2w, s_b2r = sem("s_b2w"), sem("s_b2r")
        s_xg = [sem(f"s_xg{u}") for u in range(U)]
        l_xT, l_xTc, l_h, l_relu = sem("l_xT"), sem("l_xTc"), sem("l_h"), sem("l_relu")
        l_hst, l_hvar, l_hstd, l_hrs, l_rn = sem("l_hst"), sem("l_hvar"), sem("l_hstd"), sem("l_hrs"), sem("l_rn")
        l_rT, l_rTc, l_y, l_yrelu = sem("l_rT"), sem("l_rTc"), sem("l_y"), sem("l_yrelu")
        l_yst, l_yvar, l_ystd, l_yrs, l_yn = sem("l_yst"), sem("l_yvar"), sem("l_ystd"), sem("l_yrs"), sem("l_yn")
        l_meta = sem("l_meta")
        l_yg, l_yb, l_yo = sem("l_yg"), sem("l_yb"), sem("l_yo")
        s_res = [sem(f"s_res{u}") for u in range(U)]
        s_y = [sem(f"s_y{g}") for g in range(G)]
        f_sum, f_gb, f_out, s_out = sem("f_sum"), sem("f_gb"), sem("f_out"), sem("s_out")

        class Steps:
            def __init__(self, eng, s):
                self.eng, self.sem, self.n = eng, s, 0

            def mark(self, ins):
                self.n += 1
                ins.then_inc(self.sem, 1)

            def then(self, ins):
                self.mark(ins)
                self.eng.wait_ge(self.sem, self.n)

        x_v = x.rearrange("b (c p) d -> p (b c) d", p=P)
        out_v = out.rearrange("b (c p) d -> p (b c) d", p=P)
        def tiles(eng, step, lag, kind=None):
            def row(n, t0):
                if kind is None:
                    return lambda i: None
                vals = nc.values_load_multi_w_load_instructions(
                    etab[0:1, bass.ds(n, 1), :].rearrange("p a n -> p (a n)"), engines=(kind,), min_val=0, max_val=E - 1,
                    skip_runtime_bounds_check_because="the table's entries are held to 0 ... E - 1 where it is made")[1]
                return lambda i: (lambda back: vals[i - t0 - back])

            at = row(0, 0)
            for n in range(lag, FIRST):
                step(n - lag, (n - lag) % U, (n - lag) // U, at(n - lag))
            with eng.Fori(0, ROUNDS) as j:
                at = row(j + 1, U)
                for n in range(FIRST, FIRST + U):
                    step(j * U + (n - lag), (n - lag) % U, j + (n - lag) // U, at(n - lag))
            at = row(LOOPED // U, LOOPED // U * U)
            for n in range(LOOPED, NS + 2):
                step(n - lag, (n - lag) % U, (n - lag) // U, at(n - lag))

        block = ctx.enter_context(nc.Block())

        @block.sync
        def _(sp):
            def load_x(g):
                sp.dma_start(X[:, g * TG:(g + 1) * TG, :], x_v[:, g * TG:(g + 1) * TG, :]).then_inc(s_x[g], 16)

            load_x(0)
            sp.dma_start(pa[:, :], packa).then_inc(s_pa, 16)
            sp.dma_start(cst[:, :], const).then_inc(s_cst, 16)
            load_x(1)
            sp.dma_start(bo8[:, :], bo.rearrange("(a n) -> a n", a=1).broadcast_to([B, D])).then_inc(s_bo, 16)
            sp.dma_start(pb[:, :], packb).then_inc(s_pb, 16)
            sp.dma_start(rp[:, :], rowpack).then_inc(s_rp, 16)
            load_x(2)
            load_x(3)
            sp.dma_start(brb[:, :], br.rearrange("(a n) -> a n", a=1).broadcast_to([P, E])).then_inc(s_br, 16)
            sp.dma_start(dst[:, :], dest).then_inc(s_dst, 16)
            sp.dma_start(w2[:, :, :], W2.rearrange("e (c p) d -> p (e c) d", p=P)).then_inc(s_w2, 16)
            sp.wait_ge(mod_rows, 1)
            sp.dma_start(modrows, rows[:, :, :]).then_inc(s_modw, 16)
            sp.wait_ge(s_modw, 16)
            for n, (k0, k1_) in enumerate(((0, 2), (2, 5))):
                sp.dma_start(MB[:, :, k0:k1_, :], modrows[:, k0:k1_, :].rearrange("(a b) k d -> a b k d", a=1)
                             .broadcast_to([P, B, k1_ - k0, D])).then_inc(s_modr[n], 16)
            sp.dma_start(w1[:, :, :], W1.rearrange("e d f -> d e f")).then_inc(s_w1, 16)
            for a, b in ((g2b, g2), (be2b, be2)):
                row = b.rearrange("(a e) d -> a (e d)", a=1).broadcast_to([P, E * D])
                sp.dma_start(a[:, :, :].rearrange("p e d -> p (e d)"), row).then_inc(s_g2, 16)
            sp.dma_start(pairs[E * RS:E * RS + ND * P, :], unused[E * P:(E + ND) * P, :]).then_inc(s_dummy, 16)
            sp.wait_ge(b1_split, 1)
            for k in range(3):
                sp.dma_start(b1r[k:k + 1, :, :].rearrange("a e (q n) -> a (e q) n", n=E * F // P),
                             b1s[:, k, :]).then_inc(s_b1r, 16)
            sp.wait_ge(b2_ok, 1)
            sp.dma_start(b2w[:, :], b2r.rearrange("a (q n) -> a q n", n=E * D // P)).then_inc(s_b2w, 16)
            sp.wait_ge(b2_split, 1)
            for k in range(3):
                sp.dma_start(b2p[k:k + 1, :].rearrange("a (q n) -> a q n", n=E * D // P), b2s[:, k, :]).then_inc(s_b2r, 16)
            sp.wait_ge(pads_ok, 1)
            for e in range(E):
                row = sp.value_load(padtab[0:1, e:e + 1], min_val=e * RS, max_val=e * RS + T)
                sp.dma_start(pairs[bass.ds(row, P), :], unused[e * P:(e + 1) * P, :]).then_inc(s_padded, 16)
            sp.wait_ge(etab_ok, 1)
            sp.wait_ge(s_dummy, 16)
            sp.wait_ge(s_padded, 16 * E)
            sp.wait_ge(sent, 16 * TOP * NT)

            def load(t, u):
                row = sp.value_load(rowtab[0:1, bass.ds(t, 1)], min_val=0, max_val=E * RS + (ND - 1) * P)
                if not isinstance(t, int) or t >= U:
                    sp.wait_ge(l_meta, t - (U - 1))
                sp.dma_start(XG[:, u, :], pairs[bass.ds(row, P), :]).then_inc(s_xg[u], 16)

            for n in range(U):
                load(n, n)
            with sp.Fori(1, NS // U) as j:
                for u in range(U):
                    load(j * U + u, u)
            for n in range(NS // U * U, NS):
                load(n, n % U)
            for u in range(U):
                sp.wait_ge(s_res[u], 16 * len(range(u, NS, U)))
            for g in range(G):
                for k in range(TOP):
                    sp.dma_start(Y[:, k, g * TG:(g + 1) * TG, :],
                                 results[k * T + g * TG * P:k * T + (g + 1) * TG * P, :]
                                 .rearrange("(t p) d -> p t d", p=P)).then_inc(s_y[g], 16)
            for g in range(G):
                sp.wait_ge(f_out, g + 1)
                sp.dma_start(out_v[:, g * TG:(g + 1) * TG, :], xn[:, g * TG:(g + 1) * TG, :]).then_inc(s_out, 16)
            sp.wait_ge(s_out, 16 * G)

        @block.gpsimd
        def _(gp):
            me = Steps(gp, pool)
            gp.memset(ones[:, :], 1.0).then_inc(ready, 1)
            gp.memset(onesb[:, :], 1.0).then_inc(ready, 1)
            gp.memset(eps[:, :], EPS).then_inc(ready, 1)
            gp.memset(srt[:, :, :], 0.0).then_inc(ready, 1)
            gp.wait_ge(s_cst, 16)
            me.mark(gp.tensor_copy(trib[:, :], cst[:, K_TRI:K_TRI + P]))
            gp.wait_ge(s_rp, 16)
            me.then(gp.tensor_scalar(bqk, bqk, float(S), None, ALU.mult))
            gp.wait_ge(s_pb, 16)

            def split(whole, parts, rest):
                me.then(gp.tensor_copy(parts[:, 0, :], whole))
                me.then(gp.tensor_tensor(rest[:, 0, :], whole, parts[:, 0, :], ALU.subtract))
                me.then(gp.tensor_copy(parts[:, 1, :], rest[:, 0, :]))
                me.then(gp.tensor_tensor(rest[:, 1, :], rest[:, 0, :], parts[:, 1, :], ALU.subtract))
                return gp.tensor_copy(parts[:, 2, :], rest[:, 1, :])

            split(b1w, b1s, b1t).then_inc(b1_split, 1)
            gp.wait_ge(s_dst, 16)
            for k in range(TOP):
                me.mark(gp.tensor_copy(R[:, k, :, D].bitcast(I32), dst[:, k * NT:(k + 1) * NT]))
            for g in range(G):
                gp.wait_ge(qk_cp, (g + 1) * BG)
                v = QK[0:1, g * BG:(g + 1) * BG, 0, :]
                gp.tensor_tensor(v, v, bqk.rearrange("p (a n) -> p a n", a=1).broadcast_to([1, BG, 2 * D]),
                                 ALU.add).then_inc(qk_dc, 1)
            gp.wait_ge(v_cp, 1)
            gp.tensor_tensor(BD[:, :, :, :], VT[:, :, :].rearrange("p b (a i) -> p b a i", a=1).broadcast_to([P, B, H, DK]),
                             headmask.rearrange("p (a h b) -> p a h b", a=1, b=1).broadcast_to([P, B, H, DK]),
                             ALU.mult).then_inc(bd_ok, 1)
            gp.wait_ge(s_modr[0], 16)
            for b in range(B):
                if b % BG == 0:
                    gp.wait_ge(s_x[b // BG], 16)
                gp.tensor_tensor(xga[:, b * C:(b + 1) * C, :], X[:, b * C:(b + 1) * C, :],
                                 MB[:, b, 1:2, :].broadcast_to([P, C, D]), ALU.add).then_inc(xga_ok, 1)
            gp.wait_ge(be_mm, 2)
            gp.tensor_tensor(w2[:, :, :], w2[:, :, :],
                             g1c.rearrange("p (n a) -> p n a", a=1).broadcast_to([P, E * FC, D]),
                             ALU.mult).then_inc(w2_ok, 1)
            gp.wait_ge(s_b2w, 16)
            split(b2w[:, :], b2s, b2t).then_inc(b2_split, 1)
            gp.wait_ge(pool, me.n)
            for h in range(HALF):
                gp.wait_ge(slots_ok, h + 1)
                gp.wait_ge(gates_ok, h + 1)
                gp.wait_ge(h2_copied, (h + 1) * GH)
                for i in range(h * TH, (h + 1) * TH):
                    for k in range(TOP):
                        gp.indirect_dma_start(pairs, bass.IndirectOffsetOnAxis(slots[:, i, k:k + 1], 0),
                                              R[:, k, i, :], None).then_inc(sent, 16)

            gp.wait_ge(etab_ok, 1)
            gp.wait_ge(s_g2, 32)

            def send(t, u):
                gp.indirect_dma_start(results, bass.IndirectOffsetOnAxis(meta[:, u, 0:1].bitcast(U32), 0),
                                      yo[:, u, 1, :], None).then_inc(s_res[u], 16)

            def scale(t, u, turn, expert):
                e = expert(0)
                gp.wait_ge(l_yn, t + 1)
                gp.tensor_tensor(yo[:, u, 0, :], yr[:, u, :], g2b[:, bass.ds(e, 1), :].rearrange("p a d -> p (a d)"),
                                 ALU.mult).then_inc(l_yg, 1)
                before = not isinstance(t, int) or t >= 1
                if before:
                    gp.wait_ge(l_yo, t)
                gp.wait_ge(l_yg, t + 1)
                gp.tensor_tensor(yo[:, u, 0, :], yo[:, u, 0, :], be2b[:, bass.ds(e, 1), :].rearrange("p a d -> p (a d)"),
                                 ALU.add).then_inc(l_yb, 1)
                if before:
                    send(t - 1, (u - 1) % U)

            tiles(gp, scale, 2, POOL)
            gp.wait_ge(l_yo, NS)
            send(NS - 1, (NS - 1) % U)
            for g in range(G):
                for b in range(g * BG, (g + 1) * BG):
                    gp.wait_ge(f_sum, b + 1)
                    gp.tensor_tensor(Y[:, 0, b * C:(b + 1) * C, :], Y[:, 0, b * C:(b + 1) * C, :],
                                     MB[:, b, 4:5, :].broadcast_to([P, C, D]), ALU.mult).then_inc(f_gb, 1)

        @block.scalar
        def _(ac):
            a = nc.scalar.activation
            ac.wait_ge(ready, 4)
            ac.wait_ge(s_pa, 16)
            a(sg[:, 1, :], cT, ACT.Exp, scale=-1.0).then_inc(silu_ex, 1)

            def std_first(g):
                ac.wait_ge(var1, g + 1)
                a(sd[:, g * TG:(g + 1) * TG], mv[:, g * TG:(g + 1) * TG, 1], ACT.Sqrt, bias=eps[:, :]).then_inc(std1, 1)

            std_first(0)
            for g in range(G):
                if g + 1 < G:
                    std_first(g + 1)
                if g == 0:
                    ac.wait_ge(mod_T, 1)
                for b in range(g * BG, (g + 1) * BG):
                    ac.wait_ge(hf_mm, b + 1)
                    a(HF[:, b, :], ps[:, b % 2, 0:NF], ACT.Identity, scale=modT[:, 1, b:b + 1]).then_inc(hf_cp, 1)
                for b in range((g - 1) * BG, g * BG) if g else ():
                    ac.wait_ge(qk_mm, b + 1)
                    nc.scalar.copy(QK[:, b, :, :].rearrange("p c n -> p (c n)"), ps[:, 2 + b % 2, :]).then_inc(qk_cp, 1)
            for b in range((G - 1) * BG, B):
                ac.wait_ge(qk_mm, b + 1)
                nc.scalar.copy(QK[:, b, :, :].rearrange("p c n -> p (c n)"), ps[:, 2 + b % 2, :]).then_inc(qk_cp, 1)
            ac.wait_ge(v_mm, 1)
            a(VT[:, :, :].rearrange("p b i -> p (b i)"), ps[:, 0, 0:B * DK], ACT.Identity, bias=bvc).then_inc(v_cp, 1)
            for b in range(B):
                ac.wait_ge(maxed, b // 2 * 2 + 2)
                a(srt[:, b, 0:8], mx8[:, b, :], ACT.Exp, bias=nmx[:, b:b + 1]).then_inc(topped, 1)
                a(ex[:, b, :], ps[:, 4 + b // 2, (b % 2) * S:(b % 2 + 1) * S], ACT.Exp, bias=nmx[:, b:b + 1],
                  accum_out=Z[:, b:b + 1]).then_inc(exped, 1)

            def std_second(g):
                ac.wait_ge(var2, g + 1)
                a(sd[:, g * TG:(g + 1) * TG], mv[:, g * TG:(g + 1) * TG, 1], ACT.Sqrt, bias=eps[:, :]).then_inc(std2, 1)
                ac.wait_ge(rs2_ok, g + 1)
                for t in range(g * TG, (g + 1) * TG):
                    last = a(R[:, 0, t, 0:D], x1[:, t, :], ACT.Identity, bias=nmr[:, t:t + 1], scale=rs[:, t:t + 1])
                last.then_inc(z_ok, 1)

            def turned(g):
                ac.wait_ge(h2_ok, g + 1)
                nc.scalar.copy(R[:, 1, g * TG:(g + 1) * TG, 0:D], R[:, 0, g * TG:(g + 1) * TG, 0:D]).then_inc(h2_copied, 1)
                ac.wait_ge(h2t_mm, g + 1)
                nc.scalar.copy(h2T[:, g * TG:(g + 1) * TG, :].rearrange("p t d -> p (t d)"), ps[:, g, :]).then_inc(h2t_cp, 1)

            for h in range(HALF):
                for g in range(h * GH, (h + 1) * GH):
                    std_second(g)
                for g in range(h * GH, (h + 1) * GH):
                    turned(g)
                ac.wait_ge(lg_in, h + 1)
                a(ed[:, h * TH:(h + 1) * TH], dm[:, h * TH:(h + 1) * TH], ACT.Exp).then_inc(lg_ex, 1)
            def step(t, u, turn, expert):
                late = not isinstance(t, int)
                h, w, z, y = (u - 1) % U, (u - 2) % U, (u - 3) % U, (u - 4) % U
                if late or 2 <= t < NS + 2:
                    ac.wait_ge(l_rT, t - 1)
                    nc.scalar.copy(rT[:, w % V, :, :].rearrange("p c t -> p (c t)"), ps[:, 2 + w % 2, :]).then_inc(l_rTc, 1)
                if late or 1 <= t <= NS:
                    ac.wait_ge(l_hvar, t)
                    a(hmv[:, h, 2:3], hmv[:, h, 1:2], ACT.Sqrt, bias=eps[:, :]).then_inc(l_hstd, 1)
                if late or t < NS:
                    ac.wait_ge(l_h, t + 1)
                    a(r[:, u % V, :], ps[:, u % 2, :], ACT.Relu).then_inc(l_relu, 1)
                if late or t < NS - 1:
                    turn_rows(t + 1, (u + 1) % U)
                if late or 3 <= t < NS + 3:
                    ac.wait_ge(l_yvar, t - 2)
                    a(ymv[:, z, 2:3], ymv[:, z, 1:2], ACT.Sqrt, bias=eps[:, :]).then_inc(l_ystd, 1)
                if late or t >= 4:
                    ac.wait_ge(l_yb, t - 3)
                    a(yo[:, y, 1, :], yo[:, y, 0, :], ACT.Copy, scale=meta[:, y, 1:2]).then_inc(l_yo, 1)
                if late or 2 <= t < NS + 2:
                    ac.wait_ge(l_y, t - 1)
                    a(yr[:, w, :], ps[:, 4 + w % 2, 0:D], ACT.Relu).then_inc(l_yrelu, 1)

            def turn_rows(t, u):
                ac.wait_ge(l_xT, t + 1)
                nc.scalar.copy(xT[:, u % V, :], ps[:, 6 + u % 2, 0:P]).then_inc(l_xTc, 1)

            turn_rows(0, 0)
            tiles(ac, step, 0)
            for n in range(NS + 2, NS + 4):
                step(n, n % U, n // U, None)

        @block.vector
        def _(ve):
            me = Steps(ve, dve)
            v = nc.vector

            def layernorm_stats(src, g, var, std):
                t0, t1 = g * TG, (g + 1) * TG
                for t in range(t0, t1):
                    me.mark(v.bn_stats(st[:, t, :], src[:, t, :]))
                ve.wait_ge(dve, me.n)
                for t in range(t0, t1):
                    last = v.bn_aggr(mv[:, t, :], st[:, t, :])
                last.then_inc(var, 1)
                ve.wait_ge(std, g + 1)
                me.then(v.reciprocal(rs[:, t0:t1], sd[:, t0:t1]))

            ve.wait_ge(silu_ex, 1)
            me.then(v.tensor_scalar(sg[:, 2, :], sg[:, 1, :], 1.0, None, ALU.add))
            me.then(v.reciprocal(sg[:, 3, :], sg[:, 2, :]))
            v.tensor_tensor(sg[:, 1, :], cT, sg[:, 3, :], ALU.mult).then_inc(silu, 1)

            def add_sa(g):
                b0, b1_ = g * BG, (g + 1) * BG
                ve.wait_ge(hf_cp, b1_)
                me.then(v.scalar_tensor_tensor(HF[:, b0:b1_, 0], modT[:, 0, b0:b1_], float(S), HF[:, b0:b1_, 0], ALU.mult, ALU.add))
                v.tensor_tensor(HF[:, b0:b1_, S:NF], HF[:, b0:b1_, S:NF],
                                modT[:, 0, b0:b1_].rearrange("p (b a) -> p b a", a=1).broadcast_to([P, BG, DK]),
                                ALU.add).then_inc(hf_ok, 1)

            for g in range(G):
                ve.wait_ge(s_x[g], 16)
                layernorm_stats(X, g, var1, std1)
                for t in range(g * TG, (g + 1) * TG):
                    last = v.tensor_scalar(xn[:, t, :], X[:, t, :], mv[:, t, 0:1], rs[:, t:t + 1], ALU.subtract, ALU.mult)
                last.then_inc(norm1, 1)
                if g == 0:
                    ve.wait_ge(mod_mm, 1)
                    me.mark(v.tensor_copy(modT[:, 0, :], ps[:, 7, 128:128 + B]))
                    v.tensor_scalar(modT[:, 1, :], ps[:, 7, 128 + B:128 + 2 * B], 1.0, None, ALU.add).then_inc(mod_T, 1)
                    ve.wait_ge(s_bo, 16)
                    for k, src in ((0, ps[0:B, 6, 0:D]), (4, ps[0:B, 6, 3 * D:4 * D])):
                        me.mark(v.tensor_scalar(rowt[:, 0, :], src, 0.0, 2.0, ALU.is_ge, ALU.mult))
                        me.then(v.tensor_scalar(rowt[:, 2, :], src, -1.0, 0.25, ALU.mult, ALU.max))
                        me.then(v.tensor_tensor(rowt[:, 1, :], rowt[:, 2, :], src, ALU.max))
                        me.then(v.scalar_tensor_tensor(rows[:, k, :], rowt[:, 0, :], -1.0, rowt[:, 1, :], ALU.add, ALU.mult))
                    me.mark(v.tensor_tensor(rows[:, 1, :], rows[:, 0, :], bo8[:, :], ALU.mult))
                    me.mark(v.tensor_scalar(rows[:, 2, :], ps[0:B, 6, 2 * D:3 * D], 1.0, None, ALU.add))
                    me.then(v.tensor_copy(rows[:, 3, :], ps[0:B, 6, D:2 * D]))
                    v.tensor_copy(rowt[:, 3, 0:1], rows[:, 3, 0:1]).then_inc(mod_rows, 1)
                else:
                    add_sa(g - 1)
            add_sa(G - 1)

            def corr_max(b):
                ve.wait_ge(corr, b // 2 * 2 + 2)
                me.then(v.max(mx8[:, b, :], ps[:, 4 + b // 2, (b % 2) * S:(b % 2 + 1) * S]))
                v.tensor_scalar(nmx[:, b:b + 1], mx8[:, b, 0:1], -1.0, None, ALU.mult).then_inc(maxed, 1)

            def product(g):
                b0, b1_ = g * BG, (g + 1) * BG
                ve.wait_ge(qk_dc, g + 1)
                if g:
                    ve.wait_ge(dcfix, g)
                for r_ in range(2):
                    me.mark(v.tensor_tensor(TT[:, r_, :, :, :], QK[:, b0:b1_, :, 0:D],
                                            QK[:, b0:b1_, r_:r_ + 1, D:2 * D].broadcast_to([P, BG, 2, D]), ALU.mult))
                ve.wait_ge(dve, me.n)
                me.mark(v.scalar_tensor_tensor(AD[:, b0:b1_, 0, :], TT[:, 1, :, 1, :], not0, TT[:, 0, :, 0, :], ALU.mult, ALU.add))
                me.then(v.tensor_tensor(AD[:, b0:b1_, 1, :], TT[:, 0, :, 1, :], TT[:, 1, :, 0, :], ALU.subtract))
                v.tensor_copy(AD[0:1, b0:b1_, 1, :], TT[0:1, 1, :, 1, :]).then_inc(dcfix, 1)

            def softmax_part(h):
                b0, b1_ = h * BH, (h + 1) * BH
                ve.wait_ge(topped, b1_)
                me.then(v.tensor_reduce(ovf[:, h, 0:1], srt[:, b0:b1_, 7], AX, ALU.max))
                v.tensor_scalar(ovf[:, h, 1:2], ovf[:, h, 0:1], 0.0, None, ALU.is_gt).then_inc(ovf_in, 1)
                ve.wait_ge(exped, b1_)
                me.then(v.reciprocal(rZ[:, b0:b1_], Z[:, b0:b1_]))
                ve.wait_ge(s_modr[0], 16)
                ve.wait_ge(m_mm, h + 1)
                for b in range(b0, b1_):
                    v.scalar_tensor_tensor(MM[:, b, :], ps[:, h, (b % 4) * D:(b % 4 + 1) * D], rZ[:, b:b + 1],
                                           MB[:, b, 0, :], ALU.mult, ALU.mult).then_inc(m_ok, 1)

            def sort_rest(h):
                ve.wait_ge(ovf_mm, h + 1)
                me.then(v.tensor_copy(flag[:, h:h + 1], ps[0:1, 2 + h, 0:1]))
                some = ve.value_load(flag[0:1, h:h + 1], min_val=0, max_val=P)
                with ve.If(some > 0):
                    with ve.Fori(h * BH, (h + 1) * BH) as b:
                        v.tensor_copy(work[:, 0, :], ex[:, bass.ds(b, 1), :].rearrange("p a n -> p (a n)"))
                        v.tensor_copy(top[:, :], srt[:, bass.ds(b, 1), 0:8].rearrange("p a n -> p (a n)"))
                        ve.drain()
                        with ve.Fori(0, S // 8 - 1) as k:
                            v.match_replace(work[:, 0, :], in_to_replace=top[:, :], in_values=work[:, 0, :], imm_value=-1.0)
                            ve.drain()
                            v.max(top[:, :], work[:, 0, :])
                            ve.drain()
                            v.tensor_copy(srt[:, bass.ds(b, 1), bass.ds(k * 8 + 8, 8)].rearrange("p a n -> p (a n)"), top[:, :])
                            ve.drain()
                v.memset(flag[:, h:h + 1], 0).then_inc(sorted_, 1)

            def second_norm(g):
                t0, t1 = g * TG, (g + 1) * TG
                ve.wait_ge(o_mm, g + 1)
                ve.wait_ge(xga_ok, (g + 1) * BG)
                me.then(v.tensor_tensor(x1[:, t0:t1, :].rearrange("p t d -> p (t d)"),
                                        xga[:, t0:t1, :].rearrange("p t d -> p (t d)"), ps[:, 4 + g, :], ALU.add))
                layernorm_stats(x1, g, var2, std2)
                v.scalar_tensor_tensor(nmr[:, t0:t1], mv[:, t0:t1, 0], -1.0, rs[:, t0:t1], ALU.mult, ALU.mult).then_inc(rs2_ok, 1)

            def modulate(g):
                t0, t1 = g * TG, (g + 1) * TG
                ve.wait_ge(z_ok, g + 1)
                ve.wait_ge(s_modr[1], 16)
                z = R[:, 0, t0:t1, 0:D].rearrange("p (b c) d -> p b c d", c=C)
                for k in (2, 3):
                    for b in range(g * BG, (g + 1) * BG):
                        zb = R[:, 0, b * C:(b + 1) * C, 0:D]
                        last = v.tensor_tensor(zb, zb, MB[:, b, k:k + 1, :].broadcast_to([P, C, D]),
                                               ALU.mult if k == 2 else ALU.add)
                        if k == 2:
                            me.mark(last)
                    if k == 2:
                        ve.wait_ge(dve, me.n)
                last.then_inc(h2_ok, 1)

            def route(h):
                sl = slice(h * TH, (h + 1) * TH)

                def over_e(a):
                    return a[:, sl].rearrange("p (t a) -> p t a", a=1).broadcast_to([P, TH, E])

                iotb = iota.rearrange("p (a e) -> p a e", a=1).broadcast_to([P, TH, E])

                def largest(p, m, eq, score, k, hot):
                    me.then(v.tensor_reduce(m[:, sl], p[:, sl, :], AX, ALU.max))
                    me.then(v.tensor_tensor(eq[:, sl, :], p[:, sl, :], over_e(m), ALU.is_equal))
                    me.then(v.tensor_tensor(score[:, sl, :], eq[:, sl, :], iotb, ALU.mult))
                    me.then(v.tensor_reduce(k[:, sl], score[:, sl, :], AX, ALU.max))
                    me.then(v.tensor_tensor(hot[:, sl, :], iotb, over_e(k), ALU.is_equal))

                ve.wait_ge(s_br, 16)
                ve.wait_ge(lg_mm, h + 1)
                me.then(v.tensor_tensor(lgb[:, sl, :], ps[:, 4 + 2 * h, 0:TH * E].rearrange("p (t e) -> p t e", t=TH),
                                        brb[:, :].rearrange("p (a e) -> p a e", a=1).broadcast_to([P, TH, E]), ALU.add))
                largest(lgb, m1, eq1, sc1, k1, hot1)
                me.then(v.scalar_tensor_tensor(rest[:, sl, :], hot1[:, sl, :], -3e38, lgb[:, sl, :], ALU.mult, ALU.add))
                largest(rest, m2, eq2, sc2, k2, hot2)
                me.then(v.tensor_tensor(Mb[:, sl, :], hot1[:, sl, :], hot2[:, sl, :], ALU.add))
                with nc.allow_low_precision("counts up to 16 are exact in bf16"):
                    v.tensor_reduce(Ms[:, h, :], Mb[:, sl, :].rearrange("p t e -> p e t"), AX, ALU.add).then_inc(mask_ok, 1)
                v.tensor_tensor(dm[:, sl], m2[:, sl], m1[:, sl], ALU.subtract).then_inc(lg_in, 1)
                ve.wait_ge(pos_mm, h + 1)
                me.then(v.tensor_tensor(posb[:, sl, :], ps[:, 5 + 2 * h, 0:TH * E].rearrange("p (t e) -> p t e", t=TH),
                                        cst[:, K_RS:K_RS + E].rearrange("p (a e) -> p a e", a=1).broadcast_to([P, TH, E]), ALU.add))
                for k, hot in enumerate((hot1, hot2)):
                    me.mark(v.tensor_tensor(at[k][:, sl, :], hot[:, sl, :], posb[:, sl, :], ALU.mult))
                ve.wait_ge(dve, me.n)
                for k in range(TOP):
                    me.mark(v.tensor_reduce(atf[k][:, sl], at[k][:, sl, :], AX, ALU.add))
                ve.wait_ge(dve, me.n)
                me.mark(v.tensor_copy(slots[:, sl, 0], atf[0][:, sl]))
                me.then(v.tensor_copy(slots[:, sl, 1], atf[1][:, sl]))
                v.memset(work[:, 1, 0:1], 0.0).then_inc(slots_ok, 1)
                ve.wait_ge(lg_ex, h + 1)
                me.then(v.tensor_scalar(e1[:, sl], ed[:, sl], 1.0, None, ALU.add))
                me.then(v.reciprocal(g1_[:, sl], e1[:, sl]))
                me.mark(v.tensor_copy(R[:, 0, sl, D + 1], g1_[:, sl]))
                me.then(v.tensor_tensor(R[:, 1, sl, D + 1], ed[:, sl], g1_[:, sl], ALU.mult))
                v.memset(work[:, 1, 0:1], 0.0).then_inc(gates_ok, 1)

            product(0)
            product(1)
            product(2)
            for b in range(0, BH):
                corr_max(b)
            product(3)
            ve.wait_ge(be_mm, 2)
            ve.wait_ge(s_rp, 16)
            b2v = b2r.rearrange("p (a n) -> p a n", a=2)
            v.tensor_tensor(b2v, b2v, ps[0:1, 2:4, :], ALU.add).then_inc(b2_ok, 1)
            softmax_part(0)
            for b in range(BH, B):
                corr_max(b)
            sort_rest(0)
            second_norm(0)
            second_norm(1)
            softmax_part(1)
            modulate(0)
            modulate(1)
            sort_rest(1)
            route(0)
            second_norm(2)
            second_norm(3)
            modulate(2)
            modulate(3)
            route(1)
            ve.wait_ge(cnt_mm, 1)
            cntp = ps[:, 7, 256:256 + E]
            me.mark(v.tensor_tensor(padf[:, :], ps[0:1, 7, 256:256 + E], cst[0:1, K_RS:K_RS + E], ALU.add))
            me.then(v.tensor_tensor(cmpq[:, :, :], cntp.rearrange("p (e a) -> p e a", a=1).broadcast_to([P, E, T // P]),
                                    q128.rearrange("p (a q) -> p a q", a=1).broadcast_to([P, E, T // P]), ALU.is_gt))
            me.mark(v.tensor_reduce(nt[:, 0, :], cmpq[:, :, :], AX, ALU.add))
            v.tensor_copy(padtab[:, :], padf[:, :]).then_inc(pads_ok, 1)
            ve.wait_ge(dve, me.n)
            me.then(v.tensor_tensor(cmpl[:, :, :], below, nt[:, 0:1, :].broadcast_to([P, E, E]), ALU.mult))
            me.then(v.tensor_reduce(nt[:, 1, :], cmpl[:, :, :], AX, ALU.add))
            me.then(v.tensor_tensor(nt[:, 2, :], nt[:, 1, :], nt[:, 0, :], ALU.add))
            me.then(v.tensor_tensor(cmps[:, 0, :, :], siota[0:1, :].rearrange("p (s a) -> p s a", a=1).broadcast_to([1, NE, E]),
                                    nt[0:1, 2:3, :].broadcast_to([1, NE, E]), ALU.is_ge))
            me.mark(v.tensor_tensor(cmps[:, 1, :, :], cmps[:, 0, :, :], nt[0:1, 0:1, :].broadcast_to([1, NE, E]), ALU.mult))
            me.then(v.tensor_reduce(es[:, 0, :], cmps[:, 0, :, :], AX, ALU.add))
            me.mark(v.tensor_reduce(es[:, 1, :], cmps[:, 1, :, :], AX, ALU.add))
            me.then(v.tensor_scalar(es[:, 2, :], es[:, 0, :], float(E - 1), None, ALU.min))
            for n0, width in ((0, U), (U, RW - U)):
                me.mark(v.tensor_copy(etab[:, :, n0:n0 + width],
                                      es[:, 2, n0:n0 + NR * U].rearrange("p (n u) -> p n u", u=U)[:, :, 0:width]))
            me.then(v.tensor_tensor(es[:, 3, :], siota[0:1, :], es[:, 1, :], ALU.subtract))
            me.then(v.tensor_scalar(es[:, 4, :], es[:, 0, :], float(RS // P), None, ALU.mult))
            me.then(v.tensor_tensor(es[:, 2, :], es[:, 3, :], es[:, 4, :], ALU.add))
            me.then(v.tensor_scalar(es[:, 1, :], es[:, 2, :], float(P), None, ALU.mult))
            me.then(v.tensor_copy(rowtab[:, :], es[:, 1, :]))
            v.memset(work[:, 1, 0:1], 0.0).then_inc(etab_ok, 1)

            def step(t, u, turn, expert):
                late = not isinstance(t, int)
                h, y, z = (u - 1) % U, (u - 2) % U, (u - 3) % U
                has_n, has_z = late or 1 <= t <= NS, late or t >= 3
                if has_n:
                    if has_z:
                        ve.wait_ge(l_yst, t - 2)
                    ve.wait_ge(l_hstd, t)
                    v.reciprocal(hmv[:, h, 3:4], hmv[:, h, 2:3]).then_inc(l_hrs, 1)
                elif has_z:
                    ve.wait_ge(l_yst, t - 2)
                if has_z:
                    v.bn_aggr(ymv[:, z, 0:2], yst[:, z, :]).then_inc(l_yvar, 1)
                if has_n:
                    ve.wait_ge(l_hrs, t)
                    v.tensor_scalar(r[:, h % V, :], r[:, h % V, :], hmv[:, h, 0:1], hmv[:, h, 3:4],
                                    ALU.subtract, ALU.mult).then_inc(l_rn, 1)
                has_h = late or t < NS
                if has_h:
                    ve.wait_ge(l_relu, t + 1)
                    v.bn_stats(hst[:, u, :], r[:, u % V, :]).then_inc(l_hst, 1)
                if has_z:
                    ve.wait_ge(l_ystd, t - 2)
                    v.reciprocal(ymv[:, z, 3:4], ymv[:, z, 2:3]).then_inc(l_yrs, 1)
                if has_h:
                    if late or t >= U:
                        ve.wait_ge(s_res[u], turn * 16)
                    ve.wait_ge(l_hst, t + 1)
                    v.tensor_copy(meta[:, u, :].bitcast(I32), XG[:, u, D:W].bitcast(I32)).then_inc(l_meta, 1)
                    v.bn_aggr(hmv[:, u, 0:2], hst[:, u, :]).then_inc(l_hvar, 1)
                if has_z:
                    ve.wait_ge(l_yrs, t - 2)
                    v.tensor_scalar(yr[:, z, :], yr[:, z, :], ymv[:, z, 0:1], ymv[:, z, 3:4],
                                    ALU.subtract, ALU.mult).then_inc(l_yn, 1)
                if late or 2 <= t < NS + 2:
                    ve.wait_ge(l_yrelu, t - 1)
                    v.bn_stats(yst[:, y, :], yr[:, y, :]).then_inc(l_yst, 1)

            tiles(ve, step, 0)
            step(NS + 2, (NS + 2) % U, (NS + 2) // U, None)
            def final(b):
                ve.wait_ge(f_gb, b + 1)
                ins = v.tensor_tensor(xn[:, b * C:(b + 1) * C, :], Y[:, 0, b * C:(b + 1) * C, :], x1[:, b * C:(b + 1) * C, :], ALU.add)
                if b % BG == BG - 1:
                    ins.then_inc(f_out, 1)

            for b in range(B):
                ve.wait_ge(s_y[b // BG], 32)
                v.tensor_tensor(Y[:, 0, b * C:(b + 1) * C, :], Y[:, 0, b * C:(b + 1) * C, :], Y[:, 1, b * C:(b + 1) * C, :],
                                ALU.add).then_inc(f_sum, 1)
                if b:
                    final(b - 1)
            final(B - 1)

        @block.tensor
        def _(pe):
            mm = nc.tensor.matmul
            tr = nc.tensor.transpose
            pe.wait_ge(silu, 1)
            mm(ps[:, 7, 128:128 + B], wm[:, 0:D], sg[:, 1, :], start=True, stop=True)
            mm(ps[:, 7, 128 + B:128 + 2 * B], wm[:, D:2 * D], sg[:, 1, :], start=True, stop=True)
            mm(ps[0:B, 6, :], sg[:, 1, :], wm[:, 2 * D:6 * D], start=True, stop=True).then_inc(mod_mm, 1)
            pe.wait_ge(s_cst, 16)

            def transform(b):
                pe.wait_ge(norm1, b // BG + 1)
                if b >= 2:
                    pe.wait_ge(hf_cp, b - 1)
                for c in range(C):
                    n = NF if c == 0 else S
                    ins = mm(ps[:, b % 2, 0:n], xn[:, b * C + c, :], fwd[:, c, 0:n], start=c == 0, stop=c == C - 1,
                             skip_group_check=True)
                ins.then_inc(hf_mm, 1)

            def project(b):
                if b == 0:
                    pe.wait_ge(s_pb, 16)
                pe.wait_ge(hf_ok, b // BG + 1)
                if b >= 2:
                    pe.wait_ge(qk_cp, b - 1)
                for c in range(2):
                    ins = mm(ps[:, 2 + b % 2, c * 2 * D:(c + 1) * 2 * D], HF[:, b, c * P:(c + 1) * P], wqk,
                             start=True, stop=True)
                ins.then_inc(qk_mm, 1)

            for g in range(G):
                for b in range(g * BG, (g + 1) * BG):
                    transform(b)
                for b in range((g - 1) * BG, g * BG) if g else ():
                    project(b)
            for b in range((G - 1) * BG, B):
                project(b)
            mm(ps[:, 0, 0:B * DK], wv, HF[:, :, S:NF], start=True, stop=True).then_inc(v_mm, 1)

            def correlate(b):
                pe.wait_ge(dcfix, b // BG + 1)
                for k in range(2):
                    ins = mm(ps[:, 4 + b // 2, (b % 2) * S:(b % 2 + 1) * S], AD[:, b, k, :], inv[:, k, :],
                             start=k == 0, stop=k == 1)
                ins.then_inc(corr, 1)

            def be1_w2(n):
                for e in range(n * 4, n * 4 + 4):
                    for c in range(FC):
                        ins = mm(ps[0:1, 2 + n, (e % 4) * D:(e % 4 + 1) * D], be1c[:, e * FC + c:e * FC + c + 1],
                                 w2[:, e * FC + c, :], start=c == 0, stop=c == FC - 1)
                ins.then_inc(be_mm, 1)

            def v_wo(h):
                for b in range(h * BH, (h + 1) * BH):
                    ins = mm(ps[:, h, (b % 4) * D:(b % 4 + 1) * D], BD[:, b, :, :].rearrange("p h i -> p (h i)"), wo,
                             start=True, stop=True)
                ins.then_inc(m_mm, 1)

            def above_zero(h):
                pe.wait_ge(ovf_in, h + 1)
                mm(ps[0:1, 2 + h, 0:1], ovf[:, h, 1:2], ones[:, 0:1], start=True, stop=True).then_inc(ovf_mm, 1)

            def attention_out(g):
                for i in range(g * TG, (g + 1) * TG):
                    b, c = i // C, i % C
                    ins = mm(ps[:, 4 + g, (i % TG) * D:(i % TG + 1) * D], srt[:, b, c * P:(c + 1) * P], MM[:, b, :],
                             start=True, stop=True)
                ins.then_inc(o_mm, 1)

            def logits(h):
                for g in range(h * GH, (h + 1) * GH):
                    pe.wait_ge(h2_ok, g + 1)
                    for i in range(g * TG, (g + 1) * TG):
                        ins = tr(ps[:, g, (i % TG) * D:(i % TG + 1) * D], R[:, 0, i, 0:D], ident)
                    ins.then_inc(h2t_mm, 1)
                for i in range(h * TH, (h + 1) * TH):
                    pe.wait_ge(h2t_cp, i // TG + 1)
                    ins = mm(ps[:, 4 + 2 * h, (i % TH) * E:(i % TH + 1) * E], h2T[:, i, :], wr, start=True, stop=True)
                ins.then_inc(lg_mm, 1)

            def places(h):
                pe.wait_ge(mask_ok, h + 1)
                o, t0 = ps[:, 5 + 2 * h, :], h * TH
                mm(o[:, 0:TH * E], trib[:, :], Mb[:, t0:t0 + TH, :].rearrange("p t e -> p (t e)"), start=True, stop=False,
                   skip_group_check=True)
                for j in range(h):
                    mm(o[:, 0:TH * E], onesb[:, :], Ms[:, j:j + 1, :].broadcast_to([P, TH, E]), start=False, stop=False,
                       skip_group_check=True)
                for j in range(TH - 1):
                    ins = mm(o[:, (j + 1) * E:TH * E], onesb[:, :],
                             Mb[:, t0 + j:t0 + j + 1, :].broadcast_to([P, TH - 1 - j, E]), start=False, stop=j == TH - 2,
                             skip_group_check=True)
                if h == HALF - 1:
                    for j in range(HALF):
                        ins = mm(o[:, 256:256 + E], onesb[:, :], Ms[:, j, :], start=False, stop=j == HALF - 1,
                                 skip_group_check=True)
                    ins.then_inc(cnt_mm, 1)
                    mm(o[:, 264:264 + E], onesb[:, :], Ms[:, 0, :], start=False, stop=True, skip_group_check=True).then_inc(pos_mm, 1)
                else:
                    ins.then_inc(pos_mm, 1)

            correlate(0)
            correlate(1)
            pe.wait_ge(s_w2, 16)
            pe.wait_ge(qk_cp, B)
            be1_w2(0)
            correlate(2)
            correlate(3)
            be1_w2(1)
            pe.wait_ge(bd_ok, 1)
            v_wo(0)
            v_wo(1)
            for b in range(BH, B):
                correlate(b)
            pe.wait_ge(b2_ok, 1)
            above_zero(0)
            pe.wait_ge(sorted_, 1)
            pe.wait_ge(m_ok, BH)
            attention_out(0)
            attention_out(1)
            above_zero(1)
            logits(0)
            pe.wait_ge(sorted_, 2)
            pe.wait_ge(m_ok, B)
            attention_out(2)
            attention_out(3)
            places(0)
            logits(1)
            places(1)

            pe.wait_ge(etab_ok, 1)
            pe.wait_ge(s_w1, 16)
            pe.wait_ge(w2_ok, 1)
            pe.wait_ge(s_b1r, 48)
            pe.wait_ge(s_b2r, 48)

            def turn_rows(t, u, turn):
                pe.wait_ge(s_xg[u], turn * 16 + 16)
                tr(ps[:, 6 + u % 2, 0:P], XG[:, u, 0:D], ident).then_inc(l_xT, 1)

            def step(t, u, turn, expert):
                late = not isinstance(t, int)
                w = (u - 2) % U
                has_h, has_y = late or t < NS, late or t >= 2
                if has_y:
                    ey = expert(2)
                if has_h:
                    e = expert(0)
                if has_y:
                    pe.wait_ge(l_rn, t - 1)
                    for c in range(FC):
                        ins = tr(ps[:, 2 + w % 2, c * P:(c + 1) * P], r[:, w % V, c * P:(c + 1) * P], ident)
                    ins.then_inc(l_rT, 1)
                if has_h:
                    if late or t >= 2:
                        pe.wait_ge(l_relu, t - 1)
                    mm(ps[:, u % 2, :], onesb[0:3, :], b1r[:, bass.ds(e, 1), :].rearrange("p a n -> p (a n)"), start=True, stop=False)
                    pe.wait_ge(l_xTc, t + 1)
                    mm(ps[:, u % 2, :], xT[:, u % V, :], w1[:, bass.ds(e, 1), :].rearrange("p a n -> p (a n)"),
                       start=False, stop=True).then_inc(l_h, 1)
                if late or t < NS - 1:
                    turn_rows(t + 1, (u + 1) % U, turn + (u + 1) // U)
                if has_y:
                    if late or t >= 4:
                        pe.wait_ge(l_yrelu, t - 3)
                    o = ps[:, 4 + w % 2, 0:D]
                    mm(o, onesb[0:3, :], b2p[:, bass.ds(ey * D, D)], start=True, stop=False)
                    pe.wait_ge(l_rTc, t - 1)
                    for c in range(FC):
                        ins = mm(o, rT[:, w % V, c, :], w2[:, bass.ds(ey * FC + c, 1), :].rearrange("p a d -> p (a d)"),
                                 start=False, stop=c == FC - 1)
                    ins.then_inc(l_y, 1)

            turn_rows(0, 0, 0)
            tiles(pe, step, 0, TENSOR)


def kernel(**inputs):
    from concourse import bacc
    from concourse.bass_utils import run_bass_kernel_spmd

    nc = bacc.Bacc("TRN2", target_bir_lowering=False, num_devices=1)
    a = {n.removeprefix("L0_").removeprefix("attn_").removeprefix("ffn_"):
         np.asarray(v) for n, v in inputs.items()}
    table, dest, unused = constants()
    arrays = {
        "x": a["x"],
        "packa": np.concatenate([a["c"].T, a["wmod"]], 1),
        "packb": np.concatenate([a["Wq"], a["Wk"], a["Wv"], a["Wo"], a["Wr"], a["bv"][:, None], a["g1"].reshape(E * FC, P).T,
                                 a["be1"].reshape(E * FC, P).T, a["b1"].reshape(P, E * F // P)], 1),
        "rowpack": np.concatenate([a["b2"].reshape(-1), a["bq"], a["bk"]])[None],
        "bo": a["bo"], "br": a["br"], "W1": a["W1"], "W2": a["W2"], "g2": a["g2"], "be2": a["be2"],
        "const": table, "dest": dest, "unused": unused,
    }
    arrays = {n: np.ascontiguousarray(v) for n, v in arrays.items()}
    args = [nc.dram_tensor(n, v.shape, mybir.dt.from_np(v.dtype), kind="ExternalInput").ap() for n, v in arrays.items()]
    out = nc.dram_tensor("out", [B, S, D], F32, kind="ExternalOutput").ap()
    modrows = nc.dram_tensor("modrows", [B, 5, D], F32).ap()
    pairs = nc.dram_tensor("pairs", [E * RS + ND * P, W], F32).ap()
    results = nc.dram_tensor("results", [TOP * T + (E + ND) * P, D], F32).ap()
    build(nc, *args, out, modrows, pairs, results)
    r = run_bass_kernel_spmd(nc, [arrays], core_ids=[0])
    return r.results[0]["out"]
```

```python
import numpy as np
import concourse.bass as bass
from concourse import mybir
from contextlib import ExitStack

F32 = mybir.dt.float32
BF16 = mybir.dt.bfloat16
I32 = mybir.dt.int32
U32 = mybir.dt.uint32
ALU = mybir.AluOpType
ACT = mybir.ActivationFunctionType
AX = mybir.AxisListType.X
TENSOR, VECTOR = mybir.EngineType.PE, mybir.EngineType.DVE

P = 128
B, S, D = 8, 256, 128
H, DK = 16, 8
E, F = 8, 512
TOP = 2
C = S // P
NT = B * C
G = 4
BG = B // G
TG = NT // G
T = B * S
FC = F // P
EPS = 1e-5

NS = (TOP * T + E * (P - 1)) // P
NF = S + DK

HALF = 2
BH = B // HALF
U = 6
FIRST = U + (NS - 1) % U
ROUNDS = (NS - FIRST) // U
LOOPED = FIRST + ROUNDS * U
NR = NS // U + 1
RW = U + 2
NE = NR * U + U
JP = 4
JD = 24

K_ID, K_TRI, K_INV, K_FWD = 0, P, 2 * P, 2 * P + C * S
K_HM = K_FWD + C * NF
K_IOTA = K_HM + H
K_LT = K_IOTA + E
K_Q = K_LT + E * E
K_S = K_Q + T // P
K_M0 = K_S + NE
K_P1 = K_M0 + 1
K_ROW = K_P1 + 1
K_T = K_ROW + P
K_J = K_T + NS
K_SP = K_J + NT * TOP
K_N = K_SP + NS

A_C, A_MOD, A_N = 0, B, B + 6 * D
B_QK, B_V, B_O, B_R = 0, 2 * D, 3 * D, 4 * D
B_BV = B_R + E
B_G1 = B_BV + 1
B_BE1 = B_G1 + E * FC
B_B1 = B_BE1 + E * FC
B_N = B_B1 + E * F // P


def constants():
    c = np.zeros((P, K_N), np.float64)
    c[:, K_ID:K_ID + P] = np.eye(P)
    c[:, K_TRI:K_TRI + P] = np.triu(np.ones((P, P)), 1)
    k, n = np.arange(P)[:, None], np.arange(S)[None, :]
    turn = 2 * np.pi * ((k * n) % S) / S
    sign = 1.0 - 2.0 * (np.arange(S) % 2)
    inv = np.stack([2 * np.cos(turn) / S, 2 * np.sin(turn) / S])
    inv[0, 0] = 1.0 / S
    inv[1, 0] = sign / S
    c[:, K_INV:K_INV + 2 * S] = inv.transpose(1, 0, 2).reshape(P, 2 * S)
    fwd = np.zeros((S, NF))
    fwd[:, :P] = np.cos(turn).T
    fwd[:, P:2 * P] = np.sin(turn).T
    fwd[:, P] = sign
    fwd[:DK, S:] = np.eye(DK)
    c[:, K_FWD:K_FWD + C * NF] = fwd.reshape(C, P, NF).transpose(1, 0, 2).reshape(P, C * NF)
    c[:, K_HM:K_HM + H] = np.arange(P)[:, None] // DK == np.arange(H)[None]
    c[:, K_IOTA:K_IOTA + E] = E - np.arange(E)
    c[:, K_LT:K_LT + E * E] = np.tril(np.ones((E, E)), -1).reshape(-1)
    c[:, K_Q:K_Q + T // P] = P * np.arange(T // P)
    c[:, K_S:K_S + NE] = np.arange(NE)
    c[:, K_M0] = np.arange(P) != 0
    c[:, K_P1] = 1 + np.arange(P)
    c[:, K_ROW:K_ROW + P] = np.arange(P)
    c[:, K_T:K_T + NS] = np.arange(NS)
    c[:, K_J:K_J + NT * TOP] = P * (np.arange(NT)[:, None] + NT * np.arange(TOP)[None]).reshape(-1)
    c[:, K_SP:K_SP + NS] = TOP * T + P * np.arange(NS)[None, :] + np.arange(P)[:, None] + 1
    return c.astype(np.float32)


def build(nc, x, packa, packb, rowpack, bo, br, W1, W2, g2, be2, const, out, modrows, hrows, results):
    ctx = ExitStack()
    with ctx:
        def sb(name, shape, dt=F32):
            return ctx.enter_context(nc.sbuf_tensor(name, shape, dt))

        def sem(name):
            return ctx.enter_context(nc.semaphore(name))

        cst = sb("cst", [P, K_N])
        ident = cst[:, K_ID:K_ID + P]
        inv = cst[:, K_INV:K_INV + 2 * S].rearrange("p (r n) -> p r n", r=2)
        fwd = cst[:, K_FWD:K_FWD + C * NF].rearrange("p (c n) -> p c n", c=C)
        headmask = cst[:, K_HM:K_HM + H]
        iota = cst[:, K_IOTA:K_IOTA + E]
        below = cst[:, K_LT:K_LT + E * E].rearrange("p (a b) -> p a b", a=E)
        q128 = cst[:, K_Q:K_Q + T // P]
        siota = cst[:, K_S:K_S + NE]
        not0 = cst[:, K_M0:K_M0 + 1]
        plus1 = cst[:, K_P1:K_P1 + 1]
        spare = cst[:, K_SP:K_SP + NS]

        X = sb("X", [P, NT, D])
        xn = sb("xn", [P, NT, D])
        xga = sb("xga", [P, NT, D])
        pa = sb("pa", [P, A_N])
        cT, wm = pa[:, A_C:A_C + B], pa[:, A_MOD:A_MOD + 6 * D]
        pb = sb("pb", [P, B_N])
        wqk, wv, wo, wr = (pb[:, o:o + n] for o, n in ((B_QK, 2 * D), (B_V, D), (B_O, D), (B_R, E)))
        bvc = pb[:, B_BV:B_BV + 1]
        g1c, be1c = pb[:, B_G1:B_G1 + E * FC], pb[:, B_BE1:B_BE1 + E * FC]
        b1w = pb[:, B_B1:B_B1 + E * F // P]
        rp = sb("rp", [1, E * D + 2 * D])
        b2r, bqk = rp[:, 0:E * D], rp[:, E * D:E * D + 2 * D]
        bo8 = sb("bo8", [B, D])
        brb = sb("brb", [P, E])
        w1 = sb("w1", [P, E, F])
        w2 = sb("w2", [P, E * FC, D])
        g2b = sb("g2b", [P, E, D])
        be2b = sb("be2b", [P, E, D])
        b1s = sb("b1s", [P, 3, E * F // P], BF16)
        b1t = sb("b1t", [P, 2, E * F // P])
        b1r = sb("b1r", [3, E, F], BF16)
        b2w = sb("b2w", [P, E * D // P])
        b2s = sb("b2s", [P, 3, E * D // P], BF16)
        b2t = sb("b2t", [P, 2, E * D // P])
        b2p = sb("b2p", [3, E * D], BF16)

        ones = sb("ones", [P, P])
        onesb = sb("onesb", [P, P], BF16)
        trib = sb("trib", [P, P], BF16)
        eps = sb("eps", [P, 1])
        warm, zero = sb("warm", [P, 1]), sb("zero", [P, 1], U32)

        sg = sb("sg", [P, 4, B])
        modT = sb("modT", [P, 2, B])
        rows = sb("rows", [B, 5, D])
        rowt = sb("rowt", [B, 2, 3, D])
        nmr = sb("nmr", [P, NT])
        MB = sb("MB", [P, B, 5, D])
        st = sb("st", [P, NT, 6])
        mv = sb("mv", [P, NT, 2])
        sd = sb("sd", [P, NT])
        rs = sb("rs", [P, NT])
        HF = sb("HF", [P, B, NF])
        QK = sb("QK", [P, B, 2, 2 * D])
        TT = sb("TT", [P, 2, BG, 2, D])
        AD = sb("AD", [P, B, 2, D])
        mx8 = sb("mx8", [P, B, 8])
        nmx = sb("nmx", [P, B])
        ex = xn[:, :, :].rearrange("p t d -> p (t d)").rearrange("p (b n) -> p b n", b=B)
        srt = sb("srt", [P, B, S])
        Z = sb("Z", [P, B])
        rZ = sb("rZ", [P, B])
        ovf = sb("ovf", [P, 2])
        flag = sb("flag", [1, 1], I32)
        work = sb("work", [P, 1, S])
        top = sb("top", [P, 8])
        VT = sb("VT", [P, B, DK])
        BD = sb("BD", [P, B, H, DK])
        MM = sb("MM", [P, B, D])
        H2 = sb("H2", [P, NT, D])
        h2T = X[:, :, :]
        TP = H2[:, :, :].rearrange("p t d -> p (t d)")[:, 0:4 * BG * D].rearrange("p (r b c d) -> p r b c d", r=2, b=BG, c=2)
        lgb = sb("lgb", [P, NT, E])
        lead = sb("lead", [P, NT, 8])
        eq = sb("eq", [P, NT, TOP, E])
        sc2, score, posb = (sb(n, [P, NT, E]) for n in ("sc2", "score", "posb"))
        best = sb("best", [P, NT, 8])
        hot = sb("hot", [P, NT, TOP, E])
        at = sb("at", [P, 2, NT, TOP, E])
        place, first = sb("place", [P, NT, TOP]), sb("first", [P, NT, TOP])
        placei, rowi = sb("placei", [P, NT, TOP], I32), sb("rowi", [P, NT, TOP], I32)
        rest, rown = sb("rest", [P, NT, TOP]), sb("rown", [P, NT, TOP])
        off = sb("off", [P, NT * TOP - JD, P], BF16)
        rowb, tile = sb("rowb", [P, NT, TOP], BF16), sb("tile", [P, NT, TOP], BF16)
        cb = sb("cb", [P, P + NS + NT * TOP], BF16)
        row128, tile39, pairtile = cb[:, 0:P], cb[:, P:P + NS], cb[:, P + NS:P + NS + NT * TOP]
        onerow = xn[:, :, :].rearrange("p t d -> p (t d)").bitcast(BF16).rearrange("p (j n) -> p j n", j=NT * TOP)
        onetile = HF[:, :, :].rearrange("p b n -> p (b n)")[:, 0:NT * TOP * NS // 2].bitcast(BF16).rearrange(
            "p (j n) -> p j n", j=NT * TOP)
        pairid = X[:, :, :].rearrange("p t d -> p (t d)").bitcast(BF16)[:, 0:NT * TOP * 2 * NS].rearrange(
            "p (j c n) -> p j c n", j=NT * TOP, c=2)
        tw = sb("tw", [P, 4, NS])
        token = sb("token", [P, NE], U32)
        into = sb("into", [P, NE], U32)
        dm, ed, e1 = (sb(n, [P, NT]) for n in ("dm", "ed", "e1"))
        gate = sb("gate", [P, TOP, NT])
        Mb = sb("Mb", [P, NT, E], BF16)
        nt = sb("nt", [P, 4, E])
        cmpq = sb("cmpq", [P, E, T // P])
        cmpl = sb("cmpl", [P, E, E])
        cmps = sb("cmps", [1, NE, E])
        es = sb("es", [1, 2, NE])
        etab = sb("etab", [1, NR, RW], I32)
        etab3 = sb("etab3", [1, NR, RW], I32)
        XG = sb("XG", [P, U, D])
        V = 3
        reuse = QK[:, :, :, :].rearrange("p b c n -> p (b c n)")
        r = reuse[:, 0:V * F].rearrange("p (u n) -> p u n", u=V)
        rT = reuse[:, V * F:2 * V * F].rearrange("p (u c n) -> p u c n", u=V, c=FC)
        xT = reuse[:, 2 * V * F:2 * V * F + V * P].rearrange("p (u n) -> p u n", u=V)
        src, meta = sb("src", [P, U], U32), sb("meta", [P, U], U32)
        yr = TT[:, :, :, :, :].rearrange("p r b c d -> p (r b c d)")[:, 0:U * D].rearrange("p (u d) -> p u d", u=U)
        yo = AD[:, :, :, :].rearrange("p b c n -> p (b c n)")[:, 0:U * D].rearrange("p (u d) -> p u d", u=U)
        hst = sb("hst", [P, U, 6])
        hmv = sb("hmv", [P, U, 4])
        yst = sb("yst", [P, U, 6])
        ymv = sb("ymv", [P, U, 4])
        Y = QK[:, :, :, :].rearrange("p b c n -> p (b c n)").rearrange("p (k t d) -> p k t d", k=TOP, t=NT)
        x1 = xga

        ps = ctx.enter_context(nc.psum_tensor("ps", [P, 8, 512], F32))

        s_cst, s_pa, s_pb, s_rp, s_bo, s_br = (sem(n) for n in ("s_cst", "s_pa", "s_pb", "s_rp", "s_bo", "s_br"))
        s_x = [sem(f"s_x{g}") for g in range(G)]
        s_w1, s_w2, s_g2, s_b1r = sem("s_w1"), sem("s_w2"), sem("s_g2"), sem("s_b1r")
        s_modw, s_modr = sem("s_modw"), [sem(f"s_modr{n}") for n in range(2)]
        s_h, off_ok = sem("s_h"), sem("off_ok")
        dve, act, pool = sem("dve"), sem("act"), sem("pool")
        ready = sem("ready")
        silu_ex, silu = sem("silu_ex"), sem("silu")
        mod_mm, mod_rows, mod_T = sem("mod_mm"), sem("mod_rows"), sem("mod_T")
        var1, std1, norm1 = sem("var1"), sem("std1"), sem("norm1")
        hf_mm, hf_cp, hf_ok = sem("hf_mm"), sem("hf_cp"), sem("hf_ok")
        qk_mm, qk_cp, qk_dc = sem("qk_mm"), sem("qk_cp"), sem("qk_dc")
        prod_pool, dcfix = sem("prod_pool"), sem("dcfix")
        corr, maxed, exped, topped = sem("corr"), sem("maxed"), sem("exped"), sem("topped")
        ovf_in, ovf_mm, sorted_ = sem("ovf_in"), sem("ovf_mm"), sem("sorted_")
        v_mm, v_cp, bd_ok, m_mm, m_ok = sem("v_mm"), sem("v_cp"), sem("bd_ok"), sem("m_mm"), sem("m_ok")
        o_mm, xga_ok = sem("o_mm"), sem("xga_ok")
        var2, std2, rs2_ok, z_ok, h2_last, h2_ok, h2t_mm, h2t_cp = sem("var2"), sem("std2"), sem("rs2_ok"), sem("z_ok"), sem("h2_last"), sem("h2_ok"), sem("h2t_mm"), sem("h2t_cp")
        lg_mm, lg_in, lg_ex, mask_ok, pos_mm = sem("lg_mm"), sem("lg_in"), sem("lg_ex"), sem("mask_ok"), sem("pos_mm")
        gates_ok, rows_ok, tiles_ok = sem("gates_ok"), sem("rows_ok"), sem("tiles_ok")
        id_act, id_dve, id_pool = sem("id_act"), sem("id_dve"), sem("id_pool")
        onerow_ok, onerow_act, tab_mm, token_ok, etab_ok = (sem(n) for n in (
            "onerow_ok", "onerow_act", "tab_mm", "token_ok", "etab_ok"))
        be_mm, b2_ok, w2_ok, b1_split, b2_split = sem("be_mm"), sem("b2_ok"), sem("w2_ok"), sem("b1_split"), sem("b2_split")
        s_b2w, s_b2r = sem("s_b2w"), sem("s_b2r")
        s_xg = [sem(f"s_xg{u}") for u in range(U)]
        l_xT, l_xTc, l_h, l_relu = sem("l_xT"), sem("l_xTc"), sem("l_h"), sem("l_relu")
        l_hst, l_hvar, l_hstd, l_hrs, l_rn = sem("l_hst"), sem("l_hvar"), sem("l_hstd"), sem("l_hrs"), sem("l_rn")
        l_rT, l_rTc, l_y, l_yrelu = sem("l_rT"), sem("l_rTc"), sem("l_y"), sem("l_yrelu")
        l_yst, l_yvar, l_ystd, l_yrs = sem("l_yst"), sem("l_yvar"), sem("l_ystd"), sem("l_yrs")
        l_src = sem("l_src")
        l_yg, l_yb = sem("l_yg"), sem("l_yb")
        s_res = [sem(f"s_res{u}") for u in range(U)]
        s_y = [[sem(f"s_y{k}{g}") for g in range(G)] for k in range(TOP)]
        f_gate, f_sum, f_gb, f_out, s_out = sem("f_gate"), sem("f_sum"), sem("f_gb"), sem("f_out"), sem("s_out")

        class Steps:
            def __init__(self, eng, s):
                self.eng, self.sem, self.n = eng, s, 0

            def mark(self, ins):
                self.n += 1
                ins.then_inc(self.sem, 1)

            def then(self, ins):
                self.mark(ins)
                self.eng.wait_ge(self.sem, self.n)


        def times_gb(eng, b):
            y = Y[:, 0, b * C:(b + 1) * C, :]
            return eng.tensor_tensor(y, y, MB[:, b, 4:5, :].broadcast_to([P, C, D]), ALU.mult)

        def first_pairs(eng, j0, j1):
            return eng.tensor_tensor(pairid[:, j0:j1, 1, :], onetile[:, j0:j1, :],
                                     pairtile[:, j0:j1].rearrange("p (j a) -> p j a", a=1).broadcast_to([P, j1 - j0, NS]), ALU.mult)

        def split(eng, me, whole, parts, rest):
            me.then(eng.tensor_copy(parts[:, 0, :], whole))
            me.then(eng.tensor_tensor(rest[:, 0, :], whole, parts[:, 0, :], ALU.subtract))
            me.then(eng.tensor_copy(parts[:, 1, :], rest[:, 0, :]))
            me.then(eng.tensor_tensor(rest[:, 1, :], rest[:, 0, :], parts[:, 1, :], ALU.subtract))
            return eng.tensor_copy(parts[:, 2, :], rest[:, 1, :])

        x_v = x.rearrange("b (c p) d -> p (b c) d", p=P)
        out_v = out.rearrange("b (c p) d -> p (b c) d", p=P)
        def tiles(eng, step, more, kind=None, back=0):
            table, origin = (etab3, U - 1) if back else (etab, U)

            def row(table, n, t0):
                if kind is None:
                    return lambda i: None
                vals = nc.values_load_multi_w_load_instructions(
                    table[0:1, bass.ds(n, 1), :].rearrange("p a n -> p (a n)"), engines=(kind,), min_val=0, max_val=E - 1,
                    skip_runtime_bounds_check_because="the table's entries are held to 0 ... E - 1 where it is made")[1]
                return lambda i: (lambda n: vals[i - t0 - n])

            at = row(etab, 0, 0)
            for n in range(FIRST):
                step(n, n % U, n // U, at(n))
            with eng.Fori(0, ROUNDS) as j:
                at = row(table, j + origin // U, origin)
                for n in range(FIRST, FIRST + U):
                    step(j * U + n, n % U, j + n // U, at(n))
            at = row(table, ROUNDS + origin // U, ROUNDS * U + origin)
            for n in range(LOOPED, NS + more):
                step(n, n % U, n // U, at(n))

        block = ctx.enter_context(nc.Block())

        @block.sync
        def _(sp):
            def load_x(g):
                sp.dma_start(X[:, g * TG:(g + 1) * TG, :], x_v[:, g * TG:(g + 1) * TG, :]).then_inc(s_x[g], 16)

            load_x(0)
            sp.dma_start(pa[:, :], packa).then_inc(s_pa, 16)
            sp.dma_start(cst[:, :], const).then_inc(s_cst, 16)
            load_x(1)
            sp.dma_start(bo8[:, :], bo.rearrange("(a n) -> a n", a=1).broadcast_to([B, D])).then_inc(s_bo, 16)
            sp.dma_start(pb[:, :], packb).then_inc(s_pb, 16)
            sp.dma_start(rp[:, :], rowpack).then_inc(s_rp, 16)
            load_x(2)
            load_x(3)
            sp.dma_start(brb[:, :], br.rearrange("(a n) -> a n", a=1).broadcast_to([P, E])).then_inc(s_br, 16)
            sp.dma_start(w2[:, :, :], W2.rearrange("e (c p) d -> p (e c) d", p=P)).then_inc(s_w2, 16)
            sp.wait_ge(mod_rows, 1)
            sp.dma_start(modrows, rows[:, :, :]).then_inc(s_modw, 16)
            sp.wait_ge(s_modw, 16)
            for n, (k0, k1_) in enumerate(((0, 2), (2, 5))):
                sp.dma_start(MB[:, :, k0:k1_, :], modrows[:, k0:k1_, :].rearrange("(a b) k d -> a b k d", a=1)
                             .broadcast_to([P, B, k1_ - k0, D])).then_inc(s_modr[n], 16)
            sp.dma_start(w1[:, :, :], W1.rearrange("e d f -> d e f")).then_inc(s_w1, 16)
            for a, b in ((g2b, g2), (be2b, be2)):
                row = b.rearrange("(a e) d -> a (e d)", a=1).broadcast_to([P, E * D])
                sp.dma_start(a[:, :, :].rearrange("p e d -> p (e d)"), row).then_inc(s_g2, 16)
            sp.wait_ge(b1_split, 1)
            for k in range(3):
                sp.dma_start(b1r[k:k + 1, :, :].rearrange("a e (q n) -> a (e q) n", n=E * F // P),
                             b1s[:, k, :]).then_inc(s_b1r, 16)
            for g in range(G):
                if g < G - 1:
                    sp.wait_ge(h2_ok, g + 1)
                else:
                    sp.wait_ge(h2_last, 1)
                sp.dma_start(hrows[g * TG * P:(g + 1) * TG * P, :].rearrange("(t p) d -> p t d", p=P),
                             H2[:, g * TG:(g + 1) * TG, :]).then_inc(s_h, 16)
            sp.wait_ge(b2_ok, 1)
            sp.dma_start(b2w[:, :], b2r.rearrange("a (q n) -> a q n", n=E * D // P)).then_inc(s_b2w, 16)
            sp.wait_ge(b2_split, 1)
            for k in range(3):
                sp.dma_start(b2p[k:k + 1, :].rearrange("a (q n) -> a q n", n=E * D // P), b2s[:, k, :]).then_inc(s_b2r, 16)
            for u in range(U):
                sp.wait_ge(s_res[u], 16 * len(range(u, NS, U)))
            for g in range(G):
                for k in (1, 0):
                    sp.dma_start(Y[:, k, g * TG:(g + 1) * TG, :],
                                 results[k * T + g * TG * P:k * T + (g + 1) * TG * P, :]
                                 .rearrange("(t p) d -> p t d", p=P)).then_inc(s_y[k][g], 16)
            for b in range(B):
                sp.wait_ge(f_out, b + 1)
                sp.dma_start(out_v[:, b * C:(b + 1) * C, :], xn[:, b * C:(b + 1) * C, :]).then_inc(s_out, 16)
            sp.wait_ge(s_out, 16 * B)

        @block.gpsimd
        def _(gp):
            me = Steps(gp, pool)
            gp.memset(ones[:, :], 1.0).then_inc(ready, 1)
            gp.memset(onesb[:, :], 1.0).then_inc(ready, 1)
            gp.memset(eps[:, :], EPS).then_inc(ready, 1)
            gp.memset(srt[:, :, :], 0.0).then_inc(ready, 1)
            gp.wait_ge(s_cst, 16)
            me.mark(gp.tensor_copy(trib[:, :], cst[:, K_TRI:K_TRI + P]))
            me.mark(gp.tensor_copy(cb[:, :], cst[:, K_ROW:K_SP]))
            gp.wait_ge(s_rp, 16)
            me.then(gp.tensor_scalar(bqk, bqk, float(S), None, ALU.mult))
            gp.wait_ge(s_pb, 16)
            split(gp, me, b1w, b1s, b1t).then_inc(b1_split, 1)
            me.mark(gp.memset(token[:, NS:NE], 0))
            for g in range(G):
                gp.wait_ge(qk_cp, (g + 1) * BG)
                v = QK[0:1, g * BG:(g + 1) * BG, 0, :]
                gp.tensor_tensor(v, v, bqk.rearrange("p (a n) -> p a n", a=1).broadcast_to([1, BG, 2 * D]),
                                 ALU.add).then_inc(qk_dc, 1)
            g0 = (G - 1) * BG
            gp.wait_ge(qk_dc, G)
            for r_ in range(2):
                me.mark(gp.tensor_tensor(TP[:, r_, :, :, :], QK[:, g0:B, :, 0:D],
                                         QK[:, g0:B, r_:r_ + 1, D:2 * D].broadcast_to([P, BG, 2, D]), ALU.mult))
            gp.wait_ge(pool, me.n)
            me.mark(gp.tensor_tensor(AD[:, g0:B, 0, :], TP[:, 1, :, 1, :], TP[:, 0, :, 0, :], ALU.add))
            me.then(gp.tensor_tensor(AD[:, g0:B, 1, :], TP[:, 0, :, 1, :], TP[:, 1, :, 0, :], ALU.subtract))
            gp.memset(zero[:, :], 0).then_inc(prod_pool, 1)
            gp.wait_ge(v_cp, 1)
            gp.tensor_tensor(BD[:, :, :, :], VT[:, :, :].rearrange("p b (a i) -> p b a i", a=1).broadcast_to([P, B, H, DK]),
                             headmask.rearrange("p (a h b) -> p a h b", a=1, b=1).broadcast_to([P, B, H, DK]),
                             ALU.mult).then_inc(bd_ok, 1)
            gp.wait_ge(s_modr[0], 16)
            for b in range(B):
                if b % BG == 0:
                    gp.wait_ge(s_x[b // BG], 16)
                gp.tensor_tensor(xga[:, b * C:(b + 1) * C, :], X[:, b * C:(b + 1) * C, :],
                                 MB[:, b, 1:2, :].broadcast_to([P, C, D]), ALU.add).then_inc(xga_ok, 1)
            gp.wait_ge(s_modr[1], 16)
            for g in range(G - 1):
                gp.wait_ge(z_ok, g + 1)
                for k, op in ((2, ALU.mult), (3, ALU.add)):
                    for b in range(g * BG, (g + 1) * BG):
                        hb = H2[:, b * C:(b + 1) * C, :]
                        last = gp.tensor_tensor(hb, hb, MB[:, b, k:k + 1, :].broadcast_to([P, C, D]), op)
                        if k == 2:
                            me.mark(last)
                    if k == 2:
                        gp.wait_ge(pool, me.n)
                last.then_inc(h2_ok, 1)

            gp.wait_ge(be_mm, E // 2)
            half = E * FC // 2
            gp.tensor_tensor(w2[:, half:2 * half, :], w2[:, half:2 * half, :],
                             g1c[:, half:2 * half].rearrange("p (n a) -> p n a", a=1).broadcast_to([P, half, D]),
                             ALU.mult).then_inc(w2_ok, 1)
            gp.wait_ge(tiles_ok, 1)
            first_pairs(gp, NT, NT * TOP).then_inc(id_pool, 1)

            def next_rows(t, u):
                gp.tensor_tensor(src[:, u:u + 1], token[:, bass.ds(t, 1)], zero[:, :], ALU.add).then_inc(l_src, 1)

            def gather(u):
                gp.indirect_dma_start(XG[:, u, :], None, hrows, bass.IndirectOffsetOnAxis(src[:, u:u + 1], 0)).then_inc(s_xg[u], 16)

            def send(u):
                gp.indirect_dma_start(results, bass.IndirectOffsetOnAxis(meta[:, u:u + 1], 0),
                                      yo[:, u, :], None).then_inc(s_res[u], 16)

            gp.wait_ge(pool, me.n)
            gp.wait_ge(token_ok, 1)
            gp.wait_ge(s_h, 16 * G)
            next_rows(0, 0)
            for n in range(3):
                next_rows(n + 1, n + 1)
                gp.wait_ge(l_src, n + 1)
                gather(n)

            def step(t, u, turn, expert):
                late = not isinstance(t, int)
                gathers, sends = late or t < NS - 3, late or t >= 4
                if gathers and (late or t >= 2):
                    gp.wait_ge(l_xT, t - 1)
                if gathers:
                    gp.wait_ge(l_src, t + 4)
                if sends:
                    gp.wait_ge(l_yb, t - 3)
                if late or t < NS - 4:
                    next_rows(t + 4, (u + 4) % U)
                if gathers:
                    gather((u + 3) % U)
                if sends:
                    send((u - 4) % U)

            tiles(gp, step, 4)
            for b in range(B - 1):
                gp.wait_ge(f_sum, b + 1)
                times_gb(gp, b).then_inc(f_gb, 1)

        @block.scalar
        def _(ac):
            a = nc.scalar.activation
            ac.wait_ge(ready, 3)
            a(warm[:, :], eps[:, :], ACT.Exp)
            ac.wait_ge(ready, 4)
            ac.wait_ge(s_pa, 16)
            a(sg[:, 1, :], cT, ACT.Exp, scale=-1.0).then_inc(silu_ex, 1)

            def std_first(g):
                ac.wait_ge(var1, g + 1)
                a(sd[:, g * TG:(g + 1) * TG], mv[:, g * TG:(g + 1) * TG, 1], ACT.Sqrt, bias=eps[:, :]).then_inc(std1, 1)

            std_first(0)
            for g in range(G):
                if g + 1 < G:
                    std_first(g + 1)
                if g == 0:
                    ac.wait_ge(mod_T, 1)
                for b in range(g * BG, (g + 1) * BG):
                    ac.wait_ge(hf_mm, b + 1)
                    a(HF[:, b, :], ps[:, b % 2, 0:NF], ACT.Identity, scale=modT[:, 1, b:b + 1]).then_inc(hf_cp, 1)
                for b in range((g - 1) * BG, g * BG) if g else ():
                    ac.wait_ge(qk_mm, b + 1)
                    nc.scalar.copy(QK[:, b, :, :].rearrange("p c n -> p (c n)"), ps[:, 2 + b % 2, :]).then_inc(qk_cp, 1)
            for b in range((G - 1) * BG, B):
                ac.wait_ge(qk_mm, b + 1)
                nc.scalar.copy(QK[:, b, :, :].rearrange("p c n -> p (c n)"), ps[:, 2 + b % 2, :]).then_inc(qk_cp, 1)
            ac.wait_ge(v_mm, 1)
            a(VT[:, :, :].rearrange("p b i -> p (b i)"), ps[:, 0, 0:B * DK], ACT.Identity, bias=bvc).then_inc(v_cp, 1)
            for b in range(B):
                ac.wait_ge(maxed, b // 2 * 2 + 2)
                a(srt[:, b, 0:8], mx8[:, b, :], ACT.Exp, bias=nmx[:, b:b + 1]).then_inc(topped, 1)
                a(ex[:, b, :], ps[:, 4 + b // 2, (b % 2) * S:(b % 2 + 1) * S], ACT.Exp, bias=nmx[:, b:b + 1],
                  accum_out=Z[:, b:b + 1]).then_inc(exped, 1)

            def std_second(g):
                ac.wait_ge(var2, g + 1)
                a(sd[:, g * TG:(g + 1) * TG], mv[:, g * TG:(g + 1) * TG, 1], ACT.Sqrt, bias=eps[:, :]).then_inc(std2, 1)

            def turned(g):
                ac.wait_ge(h2t_mm, g + 1)
                nc.scalar.copy(h2T[:, g * TG:(g + 1) * TG, :].rearrange("p t d -> p (t d)"), ps[:, g % 2, :]).then_inc(h2t_cp, 1)

            for g in range(G - 1):
                std_second(g)
                if g == G - 2:
                    turned(0)
                ac.wait_ge(rs2_ok, g + 1)
                for t in range(g * TG, (g + 1) * TG):
                    last = a(H2[:, t, :], x1[:, t, :], ACT.Identity, bias=nmr[:, t:t + 1], scale=rs[:, t:t + 1])
                last.then_inc(z_ok, 1)
            std_second(G - 1)
            for g in range(1, G):
                turned(g)
            ac.wait_ge(be_mm, E // 2)
            for i in range(E * FC // 2):
                last = a(w2[:, i, :], w2[:, i, :], ACT.Copy, scale=g1c[:, i:i + 1])
            last.then_inc(w2_ok, 1)
            def distance(j):
                a(off[:, j - JD, :], row128, ACT.Abs, bias=rown[:, :, :].rearrange("p t k -> p (t k)")[:, j:j + 1]).then_inc(off_ok, 1)

            def one_row(j):
                ac.wait_ge(off_ok, j - JD + 1)
                a(onerow[:, j, :], off[:, j - JD, :], ACT.Relu, bias=1.0, scale=-1.0).then_inc(onerow_act, 1)

            half = (JD + NT * TOP) // 2
            ac.wait_ge(rows_ok, 1)
            for j in range(JD, half):
                distance(j)
            for j in range(JD, half):
                one_row(j)
            ac.wait_ge(tiles_ok, 1)
            a(pairid[:, :, 0, :], onetile, ACT.Copy, scale=plus1).then_inc(id_act, 1)
            for j in range(half, NT * TOP):
                distance(j)
            for j in range(half, NT * TOP):
                one_row(j)
            ac.wait_ge(lg_in, 1)
            a(ed[:, :], dm[:, :], ACT.Exp).then_inc(lg_ex, 1)
            def step(t, u, turn, expert):
                late = not isinstance(t, int)
                h, w, z = (u - 1) % U, (u - 2) % U, (u - 3) % U
                if late or 2 <= t < NS + 2:
                    ac.wait_ge(l_rT, t - 1)
                    nc.scalar.copy(rT[:, w % V, :, :].rearrange("p c t -> p (c t)"), ps[:, 2 + w % 2, :]).then_inc(l_rTc, 1)
                if late or 1 <= t <= NS:
                    ac.wait_ge(l_hvar, t)
                    a(hmv[:, h, 2:3], hmv[:, h, 1:2], ACT.Sqrt, bias=eps[:, :]).then_inc(l_hstd, 1)
                if late or t < NS:
                    ac.wait_ge(l_h, t + 1)
                    a(r[:, u % V, :], ps[:, u % 2, :], ACT.Relu).then_inc(l_relu, 1)
                if late or t < NS - 1:
                    turn_rows(t + 1, (u + 1) % U)
                if late or 3 <= t < NS + 3:
                    ac.wait_ge(l_yvar, t - 2)
                    a(ymv[:, z, 2:3], ymv[:, z, 1:2], ACT.Sqrt, bias=eps[:, :]).then_inc(l_ystd, 1)
                if late or 2 <= t < NS + 2:
                    ac.wait_ge(l_y, t - 1)
                    a(yr[:, w, :], ps[:, 4 + w % 2, 0:D], ACT.Relu).then_inc(l_yrelu, 1)

            def turn_rows(t, u):
                ac.wait_ge(l_xT, t + 1)
                nc.scalar.copy(xT[:, u % V, :], ps[:, 6 + u % 2, 0:P]).then_inc(l_xTc, 1)

            turn_rows(0, 0)
            tiles(ac, step, 3)
            ac.wait_ge(gates_ok, 1)
            for t in range(NT):
                ac.wait_ge(s_y[1][t // TG], 16)
                a(Y[:, 1, t, :], Y[:, 1, t, :], ACT.Copy, scale=gate[:, 1, t:t + 1]).then_inc(f_gate, 1)

        @block.vector
        def _(ve):
            me = Steps(ve, dve)
            v = nc.vector

            ve.wait_ge(silu_ex, 1)
            me.then(v.tensor_scalar(sg[:, 2, :], sg[:, 1, :], 1.0, None, ALU.add))
            me.then(v.reciprocal(sg[:, 3, :], sg[:, 2, :]))
            v.tensor_tensor(sg[:, 1, :], cT, sg[:, 3, :], ALU.mult).then_inc(silu, 1)

            def add_sa(g):
                b0, b1_ = g * BG, (g + 1) * BG
                ve.wait_ge(hf_cp, b1_)
                me.then(v.scalar_tensor_tensor(HF[:, b0:b1_, 0], modT[:, 0, b0:b1_], float(S), HF[:, b0:b1_, 0], ALU.mult, ALU.add))
                v.tensor_tensor(HF[:, b0:b1_, S:NF], HF[:, b0:b1_, S:NF],
                                modT[:, 0, b0:b1_].rearrange("p (b a) -> p b a", a=1).broadcast_to([P, BG, DK]),
                                ALU.add).then_inc(hf_ok, 1)

            def first_norm(g):
                t0, t1 = g * TG, (g + 1) * TG
                ve.wait_ge(s_x[g], 16)
                for t in range(t0, t1):
                    me.mark(v.bn_stats(st[:, t, :], X[:, t, :]))
                ve.wait_ge(dve, me.n)
                for t in range(t0, t1):
                    last = v.bn_aggr(mv[:, t, :], st[:, t, :])
                last.then_inc(var1, 1)
                ve.wait_ge(std1, g + 1)
                me.then(v.reciprocal(rs[:, t0:t1], sd[:, t0:t1]))
                for t in range(t0, t1):
                    last = v.tensor_scalar(xn[:, t, :], X[:, t, :], mv[:, t, 0:1], rs[:, t:t + 1], ALU.subtract, ALU.mult)
                last.then_inc(norm1, 1)

            first_norm(0)
            ve.wait_ge(mod_mm, 1)
            me.mark(v.tensor_copy(modT[:, 0, :], ps[:, 7, 128:128 + B]))
            v.tensor_scalar(modT[:, 1, :], ps[:, 7, 128 + B:128 + 2 * B], 1.0, None, ALU.add).then_inc(mod_T, 1)
            for g in range(1, G):
                first_norm(g)
                add_sa(g - 1)
            def modulation_rows():
                ve.wait_ge(s_bo, 16)
                gates = ((0, ps[0:B, 6, 0:D]), (4, ps[0:B, 6, 3 * D:4 * D]))
                for n, (k, src) in enumerate(gates):
                    me.mark(v.tensor_scalar(rowt[:, n, 0, :], src, 0.0, 2.0, ALU.is_ge, ALU.mult))
                    me.mark(v.tensor_scalar(rowt[:, n, 2, :], src, -1.0, 0.25, ALU.mult, ALU.max))
                ve.wait_ge(dve, me.n)
                for n, (k, src) in enumerate(gates):
                    me.mark(v.tensor_tensor(rowt[:, n, 1, :], rowt[:, n, 2, :], src, ALU.max))
                ve.wait_ge(dve, me.n)
                for n, (k, src) in enumerate(gates):
                    me.mark(v.scalar_tensor_tensor(rows[:, k, :], rowt[:, n, 0, :], -1.0, rowt[:, n, 1, :], ALU.add, ALU.mult))
                me.mark(v.tensor_scalar(rows[:, 2, :], ps[0:B, 6, 2 * D:3 * D], 1.0, None, ALU.add))
                me.then(v.tensor_copy(rows[:, 3, :], ps[0:B, 6, D:2 * D]))
                v.tensor_tensor(rows[:, 1, :], rows[:, 0, :], bo8[:, :], ALU.mult).then_inc(mod_rows, 1)

            def corr_max(b):
                ve.wait_ge(corr, b + 2)
                for i in (b, b + 1):
                    me.mark(v.max(mx8[:, i, :], ps[:, 4 + b // 2, (i - b) * S:(i - b + 1) * S]))
                ve.wait_ge(dve, me.n)
                v.tensor_scalar(nmx[:, b:b + 2], mx8[:, b:b + 2, 0], -1.0, None, ALU.mult).then_inc(maxed, 2)

            def product(g):
                b0, b1_ = g * BG, (g + 1) * BG
                ve.wait_ge(qk_dc, g + 1)
                if g:
                    ve.wait_ge(dcfix, g)
                for r_ in range(2):
                    me.mark(v.tensor_tensor(TT[:, r_, :, :, :], QK[:, b0:b1_, :, 0:D],
                                            QK[:, b0:b1_, r_:r_ + 1, D:2 * D].broadcast_to([P, BG, 2, D]), ALU.mult))
                ve.wait_ge(dve, me.n)
                me.mark(v.scalar_tensor_tensor(AD[:, b0:b1_, 0, :], TT[:, 1, :, 1, :], not0, TT[:, 0, :, 0, :], ALU.mult, ALU.add))
                me.then(v.tensor_tensor(AD[:, b0:b1_, 1, :], TT[:, 0, :, 1, :], TT[:, 1, :, 0, :], ALU.subtract))
                v.tensor_copy(AD[0:1, b0:b1_, 1, :], TT[0:1, 1, :, 1, :]).then_inc(dcfix, 1)

            def overflow():
                ve.wait_ge(topped, B)
                me.then(v.tensor_reduce(ovf[:, 0:1], srt[:, :, 7], AX, ALU.max))
                v.tensor_scalar(ovf[:, 1:2], ovf[:, 0:1], 0.0, None, ALU.is_gt).then_inc(ovf_in, 1)

            def divide(h):
                b0, b1_ = h * BH, (h + 1) * BH
                ve.wait_ge(exped, b1_)
                me.then(v.reciprocal(rZ[:, b0:b1_], Z[:, b0:b1_]))
                ve.wait_ge(s_modr[0], 16)
                ve.wait_ge(m_mm, h + 1)
                for b in range(b0, b1_):
                    v.scalar_tensor_tensor(MM[:, b, :], ps[:, h, (b % 4) * D:(b % 4 + 1) * D], rZ[:, b:b + 1],
                                           MB[:, b, 0, :], ALU.mult, ALU.mult).then_inc(m_ok, 1)

            def sort_rest():
                ve.wait_ge(ovf_mm, 1)
                me.then(v.tensor_copy(flag[:, :], ps[0:1, 2, 0:1]))
                some = ve.value_load(flag[0:1, 0:1], min_val=0, max_val=P)
                with ve.If(some > 0):
                    with ve.Fori(0, B) as b:
                        v.tensor_copy(work[:, 0, :], ex[:, bass.ds(b, 1), :].rearrange("p a n -> p (a n)"))
                        v.tensor_copy(top[:, :], srt[:, bass.ds(b, 1), 0:8].rearrange("p a n -> p (a n)"))
                        ve.drain()
                        with ve.Fori(0, S // 8 - 1) as k:
                            v.match_replace(work[:, 0, :], in_to_replace=top[:, :], in_values=work[:, 0, :], imm_value=-1.0)
                            ve.drain()
                            v.max(top[:, :], work[:, 0, :])
                            ve.drain()
                            v.tensor_copy(srt[:, bass.ds(b, 1), bass.ds(k * 8 + 8, 8)].rearrange("p a n -> p (a n)"), top[:, :])
                            ve.drain()
                v.memset(flag[:, :], 0).then_inc(sorted_, 1)

            def second_norm(g):
                t0, t1 = g * TG, (g + 1) * TG
                ve.wait_ge(o_mm, g + 1)
                ve.wait_ge(xga_ok, (g + 1) * BG)
                me.then(v.tensor_tensor(x1[:, t0:t1, :].rearrange("p t d -> p (t d)"),
                                        xga[:, t0:t1, :].rearrange("p t d -> p (t d)"), ps[:, 4 + g, :], ALU.add))
                for t in range(t0, t1):
                    me.mark(v.bn_stats(st[:, t, :], x1[:, t, :]))
                ve.wait_ge(dve, me.n)
                for t in range(t0, t1):
                    last = v.bn_aggr(mv[:, t, :], st[:, t, :])
                last.then_inc(var2, 1)
                if g < G - 1:
                    ve.wait_ge(std2, g + 1)
                    me.then(v.reciprocal(rs[:, t0:t1], sd[:, t0:t1]))
                    v.scalar_tensor_tensor(nmr[:, t0:t1], mv[:, t0:t1, 0], -1.0, rs[:, t0:t1], ALU.mult, ALU.mult).then_inc(rs2_ok, 1)
                    return
                ve.wait_ge(s_modr[1], 16)
                ve.wait_ge(var2, g + 1)
                for t in range(t0, t1):
                    me.mark(v.scalar_tensor_tensor(H2[:, t, :], x1[:, t, :], mv[:, t, 0:1], MB[:, t // C, 2, :],
                                                   ALU.subtract, ALU.mult))
                ve.wait_ge(std2, g + 1)
                me.then(v.reciprocal(rs[:, t0:t1], sd[:, t0:t1]))
                for t in range(t0, t1):
                    last = v.scalar_tensor_tensor(H2[:, t, :], H2[:, t, :], rs[:, t:t + 1], MB[:, t // C, 3, :],
                                                  ALU.mult, ALU.add)
                last.then_inc(h2_last, 1)

            def route(g0, g1):
                n = (g1 - g0) * TG
                sl = slice(g0 * TG, g1 * TG)

                def over_t(a):
                    return a.rearrange("p (a e) -> p a e", a=1).broadcast_to([P, n, E])

                def over_k(a):
                    return a[:, sl].rearrange("p t (a e) -> p t a e", a=1).broadcast_to([P, n, TOP, E])

                def over_e(a):
                    return a[:, sl, 0:TOP].rearrange("p t (k a) -> p t k a", a=1).broadcast_to([P, n, TOP, E])

                ve.wait_ge(s_br, 16)
                ve.wait_ge(lg_mm, g1)
                for g in range(g0, g1):
                    gl = slice(g * TG, (g + 1) * TG)
                    me.mark(v.tensor_tensor(lgb[:, gl, :], ps[:, 4 + g, 0:TG * E].rearrange("p (t e) -> p t e", t=TG),
                                            brb[:, :].rearrange("p (a e) -> p a e", a=1).broadcast_to([P, TG, E]), ALU.add))
                ve.wait_ge(dve, me.n)
                for t in range(g0 * TG, g1 * TG):
                    me.mark(v.max(lead[:, t, :], lgb[:, t, :]))
                ve.wait_ge(dve, me.n)
                me.then(v.tensor_tensor(eq[:, sl, :, :], over_k(lgb), over_e(lead), ALU.is_equal))
                me.then(v.tensor_tensor(sc2[:, sl, :], eq[:, sl, 1, :], over_t(iota), ALU.mult))
                me.then(v.scalar_tensor_tensor(score[:, sl, :], eq[:, sl, 0, :], 2.0 * E, sc2[:, sl, :], ALU.mult, ALU.add))
                for t in range(g0 * TG, g1 * TG):
                    me.mark(v.max(best[:, t, :], score[:, t, :]))
                ve.wait_ge(dve, me.n)
                v.tensor_tensor(Mb[:, sl, :], score[:, sl, :], best[:, sl, 1:2].broadcast_to([P, n, E]), ALU.is_ge).then_inc(mask_ok, 1)
                me.mark(v.tensor_tensor(dm[:, sl], lead[:, sl, 1], lead[:, sl, 0], ALU.subtract))
                me.mark(v.tensor_tensor(hot[:, sl, :, :], over_k(score), over_e(best), ALU.is_equal))

            product(0)
            add_sa(G - 1)
            product(1)
            modulation_rows()
            product(2)
            corr_max(0)
            corr_max(2)
            ve.wait_ge(prod_pool, 1)
            me.mark(v.tensor_copy(AD[0:1, B - BG:B, 0, :], TP[0:1, 0, :, 0, :]))
            ve.wait_ge(dve, me.n)
            v.tensor_copy(AD[0:1, B - BG:B, 1, :], TP[0:1, 1, :, 1, :]).then_inc(dcfix, 1)
            corr_max(4)
            corr_max(6)
            divide(0)
            overflow()
            divide(1)
            sort_rest()
            for g in range(G):
                second_norm(g)
            route(0, 2)
            route(2, 4)
            ve.wait_ge(dve, me.n)
            v.memset(work[:, 0, 0:1], 0.0).then_inc(lg_in, 1)

            def with_hot(a, b):
                return v.tensor_tensor(at[:, a], hot[:, :, :, :], b, ALU.mult)

            ve.wait_ge(pos_mm, 1)
            me.mark(v.tensor_tensor(cmpq[:, :, :], ps[:, 0, 256:256 + E].rearrange("p (e a) -> p e a", a=1).broadcast_to([P, E, T // P]),
                                    q128.rearrange("p (a q) -> p a q", a=1).broadcast_to([P, E, T // P]), ALU.is_gt))
            me.then(with_hot(0, ps[:, 0, 0:NT * E].rearrange("p (t a e) -> p t a e", a=1, e=E).broadcast_to([P, NT, TOP, E])))
            me.mark(v.tensor_reduce(nt[:, 0, :], cmpq[:, :, :], AX, ALU.add))
            me.then(v.tensor_reduce(place[:, :, :], at[:, 0], AX, ALU.add))
            me.mark(v.tensor_tensor(cmpl[:, :, :], below, nt[:, 0:1, :].broadcast_to([P, E, E]), ALU.mult))
            me.then(v.tensor_copy(placei[:, :, :], place[:, :, :]))
            me.mark(v.tensor_reduce(nt[:, 1, :], cmpl[:, :, :], AX, ALU.add))
            me.then(v.tensor_scalar(rowi[:, :, :], placei[:, :, :], P - 1, None, ALU.bitwise_and))
            me.mark(v.tensor_scalar(rown[:, :, :], rowi[:, :, :], -1.0, None, ALU.mult))
            v.tensor_copy(rowb[:, :, :], rowi[:, :, :]).then_inc(rows_ok, 1)
            me.then(with_hot(1, nt[:, 1, :].rearrange("p (a b e) -> p a b e", a=1, b=1).broadcast_to([P, NT, TOP, E])))
            ve.wait_ge(rows_ok, 1)
            me.mark(v.tensor_tensor(rest[:, :, :], place[:, :, :], rowb[:, :, :], ALU.subtract))
            me.then(v.tensor_reduce(first[:, :, :], at[:, 1], AX, ALU.add))
            me.then(v.scalar_tensor_tensor(tile[:, :, :], rest[:, :, :], 1.0 / P, first[:, :, :], ALU.mult, ALU.add))
            v.tensor_tensor(onetile, tile[:, :, :].rearrange("p t (k a) -> p (t k) a", a=1).broadcast_to([P, NT * TOP, NS]),
                            tile39.rearrange("p (a s) -> p a s", a=1).broadcast_to([P, NT * TOP, NS]),
                            ALU.is_equal).then_inc(tiles_ok, 1)
            ve.wait_ge(tiles_ok, 1)
            first_pairs(v, 0, NT).then_inc(id_dve, 1)
            for j in range(0, JD, JP):
                v.tensor_tensor(onerow[:, j:j + JP, :], row128.rearrange("p (a r) -> p a r", a=1).broadcast_to([P, JP, P]),
                                rowb[:, :, :].rearrange("p t (k a) -> p (t k) a", a=1)[:, j:j + JP].broadcast_to([P, JP, P]),
                                ALU.is_equal).then_inc(onerow_ok, 1)
            ve.wait_ge(tab_mm, 1)
            me.then(v.tensor_reduce(tw[:, 1, :], ps[:, 1, 0:2 * NS].rearrange("p (c s) -> p s c", c=2), AX, ALU.add))
            me.mark(v.tensor_scalar(tw[:, 2, :], tw[:, 1, :], float(T), float(-T), ALU.is_gt, ALU.mult))
            me.then(v.scalar_tensor_tensor(tw[:, 3, :], tw[:, 1, :], 0.0, spare, ALU.is_equal, ALU.mult))
            me.then(v.scalar_tensor_tensor(tw[:, 0, :], tw[:, 1, :], -1.0, tw[:, 2, :], ALU.add, ALU.add))
            v.tensor_scalar(token[:, 0:NS], tw[:, 0, :], 0.0, None, ALU.max).then_inc(token_ok, 1)
            me.mark(v.scalar_tensor_tensor(into[:, 0:NS], tw[:, 1, :], -1.0, tw[:, 3, :], ALU.add, ALU.add))
            me.then(v.tensor_tensor(nt[:, 2, :], nt[:, 1, :], nt[:, 0, :], ALU.add))
            me.then(v.tensor_tensor(cmps[:, :, :], siota[0:1, :].rearrange("p (s a) -> p s a", a=1).broadcast_to([1, NE, E]),
                                    nt[0:1, 2:3, :].broadcast_to([1, NE, E]), ALU.is_ge))
            me.then(v.tensor_reduce(es[:, 0, :], cmps[:, :, :], AX, ALU.add))
            me.then(v.tensor_scalar(es[:, 1, :], es[:, 0, :], float(E - 1), None, ALU.min))
            for table, n0 in ((etab, 0), (etab3, U - 1)):
                rows_ = (NE - n0) // U - 1
                for i, width in ((0, U), (U, RW - U)):
                    last = v.tensor_copy(table[:, 0:rows_, i:i + width],
                                         es[:, 1, n0 + i:n0 + i + rows_ * U].rearrange("p (n u) -> p n u", u=U)[:, :, 0:width])
            last.then_inc(etab_ok, 1)
            ve.wait_ge(lg_ex, 1)
            me.then(v.tensor_scalar(e1[:, :], ed[:, :], 1.0, None, ALU.add))
            me.then(v.reciprocal(gate[:, 0, :], e1[:, :]))
            v.tensor_tensor(gate[:, 1, :], ed[:, :], gate[:, 0, :], ALU.mult).then_inc(gates_ok, 1)
            ve.wait_ge(be_mm, E // 2)
            ve.wait_ge(s_rp, 16)
            b2v = b2r.rearrange("p (a n) -> p a n", a=2)
            v.tensor_tensor(b2v, b2v, ps[0:1, 2:4, :], ALU.add).then_inc(b2_ok, 1)
            ve.wait_ge(s_b2w, 16)
            split(ve, me, b2w[:, :], b2s, b2t).then_inc(b2_split, 1)

            def step(t, u, turn, expert):
                late = not isinstance(t, int)
                h, y, z = (u - 1) % U, (u - 2) % U, (u - 3) % U
                has_n, has_z = late or 1 <= t <= NS, late or t >= 3
                if has_n:
                    if has_z:
                        ve.wait_ge(l_yst, t - 2)
                    ve.wait_ge(l_hstd, t)
                    v.reciprocal(hmv[:, h, 3:4], hmv[:, h, 2:3]).then_inc(l_hrs, 1)
                elif has_z:
                    ve.wait_ge(l_yst, t - 2)
                if has_z:
                    v.bn_aggr(ymv[:, z, 0:2], yst[:, z, :]).then_inc(l_yvar, 1)
                if has_n:
                    ve.wait_ge(l_hrs, t)
                    v.tensor_scalar(r[:, h % V, :], r[:, h % V, :], hmv[:, h, 0:1], hmv[:, h, 3:4],
                                    ALU.subtract, ALU.mult).then_inc(l_rn, 1)
                has_h = late or t < NS
                if has_h:
                    ve.wait_ge(l_relu, t + 1)
                    v.bn_stats(hst[:, u, :], r[:, u % V, :]).then_inc(l_hst, 1)
                if has_z:
                    ve.wait_ge(l_ystd, t - 2)
                    v.reciprocal(ymv[:, z, 3:4], ymv[:, z, 2:3]).then_inc(l_yrs, 1)
                    e = expert(3)
                    v.scalar_tensor_tensor(yr[:, z, :], yr[:, z, :], ymv[:, z, 0:1], g2b[:, bass.ds(e, 1), :].rearrange("p a d -> p (a d)"),
                                           ALU.subtract, ALU.mult).then_inc(l_yg, 1)
                if has_h:
                    if late or t >= U:
                        ve.wait_ge(s_res[u], turn * 16)
                    ve.wait_ge(l_hst, t + 1)
                    v.tensor_copy(meta[:, u:u + 1], into[:, bass.ds(t, 1)])
                    v.bn_aggr(hmv[:, u, 0:2], hst[:, u, :]).then_inc(l_hvar, 1)
                if has_z:
                    ve.wait_ge(l_yg, t - 2)
                    v.scalar_tensor_tensor(yo[:, z, :], yr[:, z, :], ymv[:, z, 3:4], be2b[:, bass.ds(e, 1), :].rearrange("p a d -> p (a d)"),
                                           ALU.mult, ALU.add).then_inc(l_yb, 1)
                if late or 2 <= t < NS + 2:
                    ve.wait_ge(l_yrelu, t - 1)
                    v.bn_stats(yst[:, y, :], yr[:, y, :]).then_inc(l_yst, 1)

            ve.wait_ge(s_g2, 32)
            tiles(ve, step, 3, VECTOR, back=3)

            def final(b):
                ve.wait_ge(f_gb, b + 1)
                v.tensor_tensor(xn[:, b * C:(b + 1) * C, :], Y[:, 0, b * C:(b + 1) * C, :], x1[:, b * C:(b + 1) * C, :],
                                ALU.add).then_inc(f_out, 1)

            for b in range(B):
                ve.wait_ge(s_y[0][b // BG], 16)
                for t in range(b * C, (b + 1) * C):
                    ve.wait_ge(f_gate, t + 1)
                    last = v.scalar_tensor_tensor(Y[:, 0, t, :], Y[:, 0, t, :], gate[:, 0, t:t + 1], Y[:, 1, t, :], ALU.mult, ALU.add)
                last.then_inc(f_sum, 1)
                if b:
                    final(b - 1)
            ve.wait_ge(f_sum, B)
            times_gb(v, B - 1).then_inc(f_gb, 1)
            final(B - 1)

        @block.tensor
        def _(pe):
            mm = nc.tensor.matmul
            tr = nc.tensor.transpose
            pe.wait_ge(silu, 1)
            mm(ps[:, 7, 128:128 + B], wm[:, 0:D], sg[:, 1, :], start=True, stop=True)
            mm(ps[:, 7, 128 + B:128 + 2 * B], wm[:, D:2 * D], sg[:, 1, :], start=True, stop=True)
            mm(ps[0:B, 6, :], sg[:, 1, :], wm[:, 2 * D:6 * D], start=True, stop=True).then_inc(mod_mm, 1)
            pe.wait_ge(s_cst, 16)

            def transform(b):
                pe.wait_ge(norm1, b // BG + 1)
                if b >= 2:
                    pe.wait_ge(hf_cp, b - 1)
                for c in range(C):
                    n = NF if c == 0 else S
                    ins = mm(ps[:, b % 2, 0:n], xn[:, b * C + c, :], fwd[:, c, 0:n], start=c == 0, stop=c == C - 1,
                             skip_group_check=True)
                ins.then_inc(hf_mm, 1)

            def project(b):
                if b == 0:
                    pe.wait_ge(s_pb, 16)
                pe.wait_ge(hf_ok, b // BG + 1)
                if b >= 2:
                    pe.wait_ge(qk_cp, b - 1)
                for c in range(2):
                    ins = mm(ps[:, 2 + b % 2, c * 2 * D:(c + 1) * 2 * D], HF[:, b, c * P:(c + 1) * P], wqk,
                             start=True, stop=True)
                ins.then_inc(qk_mm, 1)

            for g in range(G):
                for b in range(g * BG, (g + 1) * BG):
                    transform(b)
                for b in range((g - 1) * BG, g * BG) if g else ():
                    project(b)
            for b in range((G - 1) * BG, B):
                project(b)
            mm(ps[:, 0, 0:B * DK], wv, HF[:, :, S:NF], start=True, stop=True).then_inc(v_mm, 1)

            def correlate(b):
                pe.wait_ge(dcfix, b // BG + 1)
                for k in range(2):
                    ins = mm(ps[:, 4 + b // 2, (b % 2) * S:(b % 2 + 1) * S], AD[:, b, k, :], inv[:, k, :],
                             start=k == 0, stop=k == 1)
                ins.then_inc(corr, 1)

            def be1_w2(n):
                pe.wait_ge(s_w2, 16)
                pe.wait_ge(qk_cp, B)
                for e in range(2 * n, 2 * n + 2):
                    for c in range(FC):
                        ins = mm(ps[0:1, 2 + e // 4, (e % 4) * D:(e % 4 + 1) * D], be1c[:, e * FC + c:e * FC + c + 1],
                                 w2[:, e * FC + c, :], start=c == 0, stop=c == FC - 1)
                ins.then_inc(be_mm, 1)

            def v_wo(h):
                for b in range(h * BH, (h + 1) * BH):
                    ins = mm(ps[:, h, (b % 4) * D:(b % 4 + 1) * D], BD[:, b, :, :].rearrange("p h i -> p (h i)"), wo,
                             start=True, stop=True)
                ins.then_inc(m_mm, 1)

            def above_zero():
                pe.wait_ge(ovf_in, 1)
                mm(ps[0:1, 2, 0:1], ovf[:, 1:2], ones[:, 0:1], start=True, stop=True).then_inc(ovf_mm, 1)

            def attention_out(g):
                for i in range(g * TG, (g + 1) * TG):
                    b, c = i // C, i % C
                    ins = mm(ps[:, 4 + g, (i % TG) * D:(i % TG + 1) * D], srt[:, b, c * P:(c + 1) * P], MM[:, b, :],
                             start=True, stop=True)
                ins.then_inc(o_mm, 1)

            def turn(g):
                if g < G - 1:
                    pe.wait_ge(h2_ok, g + 1)
                else:
                    pe.wait_ge(h2_last, 1)
                for i in range(g * TG, (g + 1) * TG):
                    ins = tr(ps[:, g % 2, (i % TG) * D:(i % TG + 1) * D], H2[:, i, :], ident)
                ins.then_inc(h2t_mm, 1)

            def logits(g):
                pe.wait_ge(h2t_cp, g + 1)
                for i in range(g * TG, (g + 1) * TG):
                    ins = mm(ps[:, 4 + g, (i % TG) * E:(i % TG + 1) * E], h2T[:, i, :], wr, start=True, stop=True)
                ins.then_inc(lg_mm, 1)

            def places():
                o = ps[:, 0, 0:NT * E]
                for n, (t0, t1) in enumerate(((0, 2 * TG), (2 * TG, NT))):
                    pe.wait_ge(mask_ok, n + 1)
                    mm(o[:, t0 * E:t1 * E], trib[:, :], Mb[:, t0:t1, :].rearrange("p t e -> p (t e)"), start=n == 0, stop=False,
                       skip_group_check=True)
                    for j in range(t0, t1):
                        if j < NT - 1:
                            mm(o[:, (j + 1) * E:NT * E], onesb[:, :], Mb[:, j:j + 1, :].broadcast_to([P, NT - 1 - j, E]),
                               start=False, stop=j == NT - 2, skip_group_check=True)
                        ins = mm(ps[:, 0, 256:256 + E], onesb[:, :], Mb[:, j, :], start=False, stop=j == NT - 1,
                                 skip_group_check=True)
                ins.then_inc(pos_mm, 1)

            def slot_table():
                pe.wait_ge(id_act, 1)
                pe.wait_ge(id_dve, 1)
                for j in range(NT * TOP):
                    if j == NT:
                        pe.wait_ge(id_pool, 1)
                    if j >= JD:
                        pe.wait_ge(onerow_act, j - JD + 1)
                    elif j % JP == 0:
                        pe.wait_ge(onerow_ok, j // JP + 1)
                    ins = mm(ps[:, 1, 0:2 * NS], onerow[:, j, :], pairid[:, j, :, :].rearrange("p c n -> p (c n)"),
                             start=j == 0, stop=j == NT * TOP - 1)
                ins.then_inc(tab_mm, 1)

            correlate(0)
            correlate(1)
            correlate(2)
            correlate(3)
            correlate(4)
            correlate(5)
            correlate(6)
            correlate(7)
            pe.wait_ge(bd_ok, 1)
            v_wo(0)
            v_wo(1)
            be1_w2(2)
            above_zero()
            be1_w2(3)
            pe.wait_ge(sorted_, 1)
            pe.wait_ge(m_ok, B)
            for g in range(G):
                attention_out(g)
            be1_w2(0)
            be1_w2(1)
            turn(0)
            logits(0)
            turn(1)
            logits(1)
            turn(2)
            turn(3)
            logits(2)
            logits(3)
            places()
            slot_table()

            pe.wait_ge(etab_ok, 1)
            pe.wait_ge(s_w1, 16)
            pe.wait_ge(s_b1r, 48)

            def turn_rows(t, u, turn):
                pe.wait_ge(s_xg[u], turn * 16 + 16)
                tr(ps[:, 6 + u % 2, 0:P], XG[:, u, 0:D], ident).then_inc(l_xT, 1)

            def step(t, u, turn, expert):
                late = not isinstance(t, int)
                w = (u - 2) % U
                has_h, has_y = late or t < NS, late or t >= 2
                if has_y:
                    ey = expert(2)
                if has_h:
                    e = expert(0)
                if has_y:
                    pe.wait_ge(l_rn, t - 1)
                    for c in range(FC):
                        ins = tr(ps[:, 2 + w % 2, c * P:(c + 1) * P], r[:, w % V, c * P:(c + 1) * P], ident)
                    ins.then_inc(l_rT, 1)
                if has_h:
                    if late or t >= 2:
                        pe.wait_ge(l_relu, t - 1)
                    mm(ps[:, u % 2, :], onesb[0:3, :], b1r[:, bass.ds(e, 1), :].rearrange("p a n -> p (a n)"), start=True, stop=False)
                    pe.wait_ge(l_xTc, t + 1)
                    mm(ps[:, u % 2, :], xT[:, u % V, :], w1[:, bass.ds(e, 1), :].rearrange("p a n -> p (a n)"),
                       start=False, stop=True).then_inc(l_h, 1)
                if late or t < NS - 1:
                    turn_rows(t + 1, (u + 1) % U, turn + (u + 1) // U)
                if has_y:
                    if late or t >= 4:
                        pe.wait_ge(l_yrelu, t - 3)
                    if not late and t == 2:
                        pe.wait_ge(w2_ok, 2)
                        pe.wait_ge(s_b2r, 48)
                    o = ps[:, 4 + w % 2, 0:D]
                    mm(o, onesb[0:3, :], b2p[:, bass.ds(ey * D, D)], start=True, stop=False)
                    pe.wait_ge(l_rTc, t - 1)
                    for c in range(FC):
                        ins = mm(o, rT[:, w % V, c, :], w2[:, bass.ds(ey * FC + c, 1), :].rearrange("p a d -> p (a d)"),
                                 start=False, stop=c == FC - 1)
                    ins.then_inc(l_y, 1)

            turn_rows(0, 0, 0)
            tiles(pe, step, 2, TENSOR)


def kernel(**inputs):
    from concourse import bacc
    from concourse.bass_utils import run_bass_kernel_spmd

    nc = bacc.Bacc("TRN2", target_bir_lowering=False, num_devices=1)
    a = {n.removeprefix("L0_").removeprefix("attn_").removeprefix("ffn_"):
         np.asarray(v) for n, v in inputs.items()}
    table = constants()
    arrays = {
        "x": a["x"],
        "packa": np.concatenate([a["c"].T, a["wmod"]], 1),
        "packb": np.concatenate([a["Wq"], a["Wk"], a["Wv"], a["Wo"], a["Wr"], a["bv"][:, None], a["g1"].reshape(E * FC, P).T,
                                 a["be1"].reshape(E * FC, P).T, a["b1"].reshape(P, E * F // P)], 1),
        "rowpack": np.concatenate([a["b2"].reshape(-1), a["bq"], a["bk"]])[None],
        "bo": a["bo"], "br": a["br"], "W1": a["W1"], "W2": a["W2"], "g2": a["g2"], "be2": a["be2"],
        "const": table,
    }
    arrays = {n: np.ascontiguousarray(v) for n, v in arrays.items()}
    args = [nc.dram_tensor(n, v.shape, mybir.dt.from_np(v.dtype), kind="ExternalInput").ap() for n, v in arrays.items()]
    out = nc.dram_tensor("out", [B, S, D], F32, kind="ExternalOutput").ap()
    modrows = nc.dram_tensor("modrows", [B, 5, D], F32).ap()
    hrows = nc.dram_tensor("hrows", [T, D], F32).ap()
    results = nc.dram_tensor("results", [TOP * T + NS * P, D], F32).ap()
    build(nc, *args, out, modrows, hrows, results)
    r = run_bass_kernel_spmd(nc, [arrays], core_ids=[0])
    return r.results[0]["out"]
```
